# Optimizing a Trainium2 kernel written in Bass

```python
import numpy as np
import jax
import jax.numpy as jnp

def _softmax(x, axis=-1):
    return jax.nn.softmax(x, axis=axis)

def _gelu(x):
    return jax.nn.gelu(x, approximate=True)

def _silu(x):
    return jax.nn.silu(x)

def _sigmoid(x):
    return jax.nn.sigmoid(x)

def _layernorm(x, axis=-1, eps=1e-05):
    m = jnp.mean(x, axis=axis, keepdims=True)
    v = jnp.var(x, axis=axis, keepdims=True)
    return (x - m) / jnp.sqrt(v + eps)

def _scatter_add(tgt, idx, src, axis=0):
    return tgt.at[idx].add(src)

def _segment_sum(src, seg, n):
    return jax.ops.segment_sum(src, seg, n)
kernel_name = 'mk_cond_resid_d2_seqx_r4_274de9'

def setup_inputs(seed: int=0):
    np.random.seed(seed)
    _w = jnp.asarray

    def _rec_inputs():
        import jax
        import jax.numpy as jnp
        _rk = jax.random.key(seed)
        x = -0.000125 + 0.9999 * jax.random.normal(jax.random.fold_in(_rk, 1), (4, 512, 512), jnp.float32)
        _lenS = 512 - jax.random.randint(jax.random.fold_in(_rk, 7), (4,), 0, max(1, 512 // 4) + 1, jnp.int32)
        _lenS2 = 512 - jax.random.randint(jax.random.fold_in(_rk, 8), (4,), 0, max(1, 512 // 4) + 1, jnp.int32)
        cond_2048 = 7.82532e-05 + 0.0100527 * jax.random.normal(jax.random.fold_in(_rk, 11), (4, 512), jnp.float32)
        return (x, cond_2048)
    x, cond_2048 = _rec_inputs()

    def _L0_cond_setup():
        import jax, jax.numpy as jnp
        import numpy as np
        NUM_BLOCKS = 8
        NUM_LAYERS = 4
        EPS = 1e-06
        key = jax.random.key(seed)
        ks = jax.random.split(key, 6)
        B, S, H = (4, 1024, 512)
        inputs = jax.random.normal(ks[0], (B, S, H), dtype=jnp.float32)
        query_vectors = jax.random.normal(ks[1], (NUM_LAYERS, H), dtype=jnp.float32) * 0.01
        lim = float(np.sqrt(6.0 / (H + H)))
        Wk = jax.random.uniform(ks[2], (H, H), minval=-lim, maxval=lim, dtype=jnp.float32)
        Wo = jax.random.uniform(ks[3], (H, H), minval=-lim, maxval=lim, dtype=jnp.float32)
        rms_weight = jnp.ones((H,), dtype=jnp.float32)
        ln_gamma = jnp.ones((H,), dtype=jnp.float32)
        ln_beta = jnp.zeros((H,), dtype=jnp.float32)
        return {'inputs': inputs, 'layer_idx': 1, 'rms_weight': rms_weight, 'query_vectors': query_vectors, 'Wk': Wk, 'Wo': Wo, 'ln_gamma': ln_gamma, 'ln_beta': ln_beta}
    _L0_cond_all = _L0_cond_setup()
    _L0_cond_in = {k: v for k, v in _L0_cond_all.items() if k in ('rms_weight', 'Wk', 'Wo', 'ln_gamma', 'ln_beta')}
    del _L0_cond_all

    def _L1_cond_setup():
        import jax, jax.numpy as jnp
        import numpy as np
        DIM = 512
        H = 16
        DH = 128
        INNER = H * DH
        MLP = 4 * DIM
        B, T = (2, 512)
        EPS = 1e-06

        def _ln(x):
            mu = jnp.mean(x, axis=-1, keepdims=True)
            var = jnp.var(x, axis=-1, keepdims=True)
            return (x - mu) * jax.lax.rsqrt(var + EPS)
        key = jax.random.key(seed)
        ks = jax.random.split(key, 12)
        s = 0.02
        return {'x': jax.random.normal(ks[0], (B, T, DIM), jnp.float32), 'timestep_embed': jax.random.normal(ks[1], (B, DIM), jnp.float32), 'ada_w': jax.random.normal(ks[2], (DIM, 6 * DIM), jnp.float32) * s, 'ada_b': jnp.zeros((6 * DIM,), jnp.float32), 'qkv_w': jax.random.normal(ks[3], (DIM, 3 * INNER), jnp.float32) * s, 'qkv_b': jnp.zeros((3 * INNER,), jnp.float32), 'out_w': jax.random.normal(ks[4], (INNER, DIM), jnp.float32) * s, 'out_b': jnp.zeros((DIM,), jnp.float32), 'ffn_w1': jax.random.normal(ks[5], (DIM, MLP), jnp.float32) * s, 'ffn_b1': jnp.zeros((MLP,), jnp.float32), 'ffn_w2': jax.random.normal(ks[6], (MLP, DIM), jnp.float32) * s, 'ffn_b2': jnp.zeros((DIM,), jnp.float32)}
    _L1_cond_all = _L1_cond_setup()
    _L1_cond_in = {k: v for k, v in _L1_cond_all.items() if k in ('ada_w', 'ada_b', 'qkv_w', 'qkv_b', 'out_w', 'out_b', 'ffn_w1', 'ffn_b1', 'ffn_w2', 'ffn_b2')}
    del _L1_cond_all
    return {'x': x, 'cond_2048': cond_2048, 'L0_cond_rms_weight': _L0_cond_in['rms_weight'], 'L0_cond_Wk': _L0_cond_in['Wk'], 'L0_cond_Wo': _L0_cond_in['Wo'], 'L0_cond_ln_gamma': _L0_cond_in['ln_gamma'], 'L0_cond_ln_beta': _L0_cond_in['ln_beta'], 'L1_cond_ada_w': _L1_cond_in['ada_w'], 'L1_cond_ada_b': _L1_cond_in['ada_b'], 'L1_cond_qkv_w': _L1_cond_in['qkv_w'], 'L1_cond_qkv_b': _L1_cond_in['qkv_b'], 'L1_cond_out_w': _L1_cond_in['out_w'], 'L1_cond_out_b': _L1_cond_in['out_b'], 'L1_cond_ffn_w1': _L1_cond_in['ffn_w1'], 'L1_cond_ffn_b1': _L1_cond_in['ffn_b1'], 'L1_cond_ffn_w2': _L1_cond_in['ffn_w2'], 'L1_cond_ffn_b2': _L1_cond_in['ffn_b2']}

def reference(x, cond_2048, L0_cond_rms_weight, L0_cond_Wk, L0_cond_Wo, L0_cond_ln_gamma, L0_cond_ln_beta, L1_cond_ada_w, L1_cond_ada_b, L1_cond_qkv_w, L1_cond_qkv_b, L1_cond_out_w, L1_cond_out_b, L1_cond_ffn_w1, L1_cond_ffn_b1, L1_cond_ffn_w2, L1_cond_ffn_b2):
    import jax
    import jax.numpy as jnp

    def _L0_cond_ref(inputs, layer_idx, rms_weight, query_vectors, Wk, Wo, ln_gamma, ln_beta):
        import jax, jax.numpy as jnp
        import numpy as np
        NUM_BLOCKS = 8
        NUM_LAYERS = 4
        EPS = 1e-06
        B, S, H = inputs.shape
        block_size = max(1, S // NUM_BLOCKS)
        n_blocks = S // block_size
        block_repr = inputs.reshape(B, n_blocks, block_size, H).sum(axis=2)
        keys = jnp.einsum('bnh,kh->bnk', block_repr, Wk)
        rms = jnp.sqrt(jnp.mean(keys * keys, axis=-1, keepdims=True) + EPS)
        keys = keys / rms * rms_weight
        q = query_vectors[layer_idx]
        scores = jnp.einsum('bnh,h->bn', keys, q)
        attn = jax.nn.softmax(scores, axis=-1)
        attended = jnp.einsum('bn,bnh->bh', attn, block_repr)
        attended = jnp.broadcast_to(attended[:, None, :], (B, S, H))
        proj = jnp.einsum('bsh,kh->bsk', attended, Wo)
        x = inputs + proj
        mu = jnp.mean(x, axis=-1, keepdims=True)
        var = jnp.mean((x - mu) ** 2, axis=-1, keepdims=True)
        out = (x - mu) / jnp.sqrt(var + EPS) * ln_gamma + ln_beta
        return out

    def _L1_cond_ref(x, timestep_embed, ada_w, ada_b, qkv_w, qkv_b, out_w, out_b, ffn_w1, ffn_b1, ffn_w2, ffn_b2):
        import jax, jax.numpy as jnp
        import numpy as np
        DIM = 512
        H = 16
        DH = 128
        INNER = H * DH
        MLP = 4 * DIM
        B, T = (2, 512)
        EPS = 1e-06

        def _ln(x):
            mu = jnp.mean(x, axis=-1, keepdims=True)
            var = jnp.var(x, axis=-1, keepdims=True)
            return (x - mu) * jax.lax.rsqrt(var + EPS)
        Bc, Tc, D = x.shape
        ada = (timestep_embed @ ada_w + ada_b)[:, None, :]
        shift1, scale1, gate1, shift2, scale2, gate2 = jnp.split(ada, 6, axis=-1)
        x1 = _ln(x) * (1.0 + scale1) + shift1
        qkv = (x1 @ qkv_w + qkv_b).reshape(Bc, Tc, 3, H, DH)
        q, k, v = (qkv[:, :, 0], qkv[:, :, 1], qkv[:, :, 2])
        scale = DH ** (-0.5)
        attn = jnp.einsum('bthd,bshd->bhts', q, k) * scale
        attn = jax.nn.softmax(attn, axis=-1)
        attn_out = jnp.einsum('bhts,bshd->bthd', attn, v).reshape(Bc, Tc, INNER)
        attn_out = attn_out @ out_w + out_b
        x = x + gate1 * attn_out
        x2 = _ln(x) * (1.0 + scale2) + shift2
        h = jax.nn.gelu(x2 @ ffn_w1 + ffn_b1, approximate=False)
        x = x + gate2 * (h @ ffn_w2 + ffn_b2)
        return x
    x = x + _L0_cond_ref(x, 1, L0_cond_rms_weight, cond_2048, L0_cond_Wk, L0_cond_Wo, L0_cond_ln_gamma, L0_cond_ln_beta)
    x = x + _L1_cond_ref(x, cond_2048, L1_cond_ada_w, L1_cond_ada_b, L1_cond_qkv_w, L1_cond_qkv_b, L1_cond_out_w, L1_cond_out_b, L1_cond_ffn_w1, L1_cond_ffn_b1, L1_cond_ffn_w2, L1_cond_ffn_b2)
    return x

_drawn_inputs = setup_inputs


def setup_inputs(seed=0):
    import zlib

    import numpy as np

    out = dict(_drawn_inputs(seed))
    spreads = {'L0_cond_rms_weight': (1.0, 0.6),
     'L0_cond_ln_gamma': (1.0, 0.2),
     'L0_cond_ln_beta': (0.0, 0.1),
     'L1_cond_ada_b': (0.0, 0.733),
     'L1_cond_qkv_b': (0.0, 0.8),
     'L1_cond_out_b': (0.0, 2.0),
     'L1_cond_ffn_b1': (0.0, 0.8),
     'L1_cond_ffn_b2': (0.0, 2.0)}
    factors = {'L1_cond_ada_w': 8.0,
     'L1_cond_qkv_w': 7.966,
     'L1_cond_out_w': 7.738,
     'L1_cond_ffn_w1': 8.0,
     'L1_cond_ffn_w2': 7.795}
    for name, (base, spread) in spreads.items():
        noise = np.random.default_rng([zlib.crc32(name.encode()), seed]).standard_normal(out[name].shape)
        drawn = base * np.exp(spread * noise) if base else spread * noise
        out[name] = jnp.asarray(drawn.astype(out[name].dtype))
    for name, factor in factors.items():
        out[name] = (out[name] * factor).astype(out[name].dtype)
    return out
```

```python
from contextlib import ExitStack

import concourse.bass as bass
from concourse import mybir

F32 = mybir.dt.float32
F32R = mybir.dt.float32r
ACT = mybir.ActivationFunctionType
ALU = mybir.AluOpType
AX_X = mybir.AxisListType.X

P = 128
B = 4
S = 512
D = 512
KT = D // P
TT = S // P
H = 16
DH = 128
HG = 4
G = H // HG
MLP = 2048
JG = MLP // 512
NBLK = 8
BLK = S // NBLK
SCALE = float(DH) ** -0.5
EPS = 1e-6
HI, LO = 0, 1
MQ, MK, MV, MO = 0, 1, 2, 3
PAIRS = ((HI, HI), (HI, LO), (LO, HI))

NORM_ORDER = (2, 3, 0, 1)

SLOTS = B * HG


def group_order():
    steps = [("K", 0, 0, 4), ("Q", 0, 0, 4)] + [("V", 0, j) for j in range(TT)]
    steps += [("S", 0, t) for t in range(TT)]
    for n in range(SLOTS):
        if n < SLOTS - 1:
            steps += [("K", n + 1, 0, 4), ("C", n, 0), ("Q", n + 1, 0, 2), ("C", n, 1),
                      ("Q", n + 1, 2, 4), ("C", n, 2), ("C", n, 3)]
        else:
            steps += [("C", n, j) for j in range(TT)]
        if n % HG == 0 and n:
            steps += [("V", n // HG, j) for j in range(TT)]
            steps += [("Y", n // HG - 1, i) for i in range(TT)]
        if n < SLOTS - 1:
            steps += [("D", n, 0), ("S", n + 1, 0), ("S", n + 1, 1), ("D", n, 1), ("S", n + 1, 2), ("D", n, 2),
                      ("S", n + 1, 3), ("D", n, 3)]
        else:
            steps += [("D", n, j) for j in range(TT)]
    steps += [("Y", B - 1, i) for i in range(TT)]
    return steps


ORDER = group_order()


def finished():
    out = []
    for s in ORDER:
        if s[0] in "KQ" and s[3] == KT:
            out.append((s[0], s[1]))
        elif s[0] == "D" and s[2] == TT - 1:
            out.append(("O", s[1]))
        elif s[0] in "VYSC":
            out.append(s)
    return out


DONE = finished()
M_TILES = [t for t in DONE if t[0] in "KQVOY"]
M_AT = {t: k for k, t in enumerate(M_TILES)}
NM = len(M_TILES)
SPLIT_AT = {t: k for k, t in enumerate(t for t in M_TILES if t[0] != "Y")}
NSPLIT = len(SPLIT_AT)
NS = SLOTS * TT
assert NM % 4 == 0


def build(nc, x, cond, rms_w, Wk, Wo, gamma, beta, ada_w, ada_b, qkv_w, qkv_b, out_w, out_b,
          ffn_w1, ffn_b1, ffn_w2, ffn_b2, out):
    ctx = ExitStack()
    with ctx:
        def sb(name, shape, dt=F32, stack=ctx):
            return stack.enter_context(nc.sbuf_tensor(name, shape, dt))

        def sem(name):
            return ctx.enter_context(nc.semaphore(name))

        x_mid = nc.dram_tensor("x_mid", (B, S, D), F32, kind="Internal").ap()
        xx_mid = nc.dram_tensor("xx_mid", (B, S, D), F32, kind="Internal").ap()
        xT_mid = [nc.dram_tensor(f"xT_mid{n}", (B, P, 2 * KT * S), F32, kind="Internal").ap() for n in range(2)]
        ada_mid = nc.dram_tensor("ada_mid", (B, 6 * D), F32, kind="Internal").ap()

        acc = sb("acc", [P, B * TT, D])
        xT = sb("xT", [P, 2, 2, KT, S], F32R)
        W = sb("W", [P, 4, 2, 4, 512], F32R)
        raw = sb("raw", [P, 4, 512])
        prob = sb("prob", [P, TT, S])
        ident = sb("ident", [P, P])
        cols = sb("cols", [P, 64])
        group_cols = sb("group_cols", [P, 12])
        block_ind = sb("block_ind", [P, 62])
        batch_mask = sb("batch_mask", [32, B])
        one = sb("one", [1, 1])
        eps = sb("eps", [P, 1])
        condT = sb("condT", [P, KT, B])
        ada_cols = sb("ada_cols", [P, 4, KT, B])
        neg_max = sb("neg_max", [P, TT])
        row_sum = sb("row_sum", [P, TT])
        row_inv = sb("row_inv", [P, TT])
        stats = sb("stats", [P, TT, 6])
        mean_var = sb("mean_var", [P, TT, 2])
        std = sb("std", [P, TT])
        rstd = sb("rstd", [P, TT])
        shift = sb("shift", [P, TT])
        small = sb("small", [32, 16])
        small_row = sb("small_row", [1, 96])
        cond_sb = sb("cond_sb", [B, D])
        bias_rows = sb("bias_rows", [64, P])
        blocks = sb("blocks", [32, D])
        blocksT = sb("blocksT", [P, KT, 32])

        pro = ExitStack()
        WkT = sb("WkT", [P, KT, D], stack=pro)
        WoT = sb("WoT", [P, KT, D], stack=pro)
        Wk_sb = sb("Wk_sb", [P, KT, D], stack=pro)
        Wo_sb = sb("Wo_sb", [P, KT, D], stack=pro)
        ada = sb("ada", [B, 6 * D], stack=pro)
        raw2 = sb("raw2", [P, 4, 512], stack=pro)
        affine = sb("affine", [P, 2, D], stack=pro)
        pro.close()
        att_bc = Wk_sb[:, :, :].rearrange("p k (b c) -> p k b c", b=B)
        mid = ExitStack()
        gate1 = sb("gate1", [P, B, D], stack=mid)
        x_in = sb("x_in", [P, B * TT, D], stack=mid)
        mid_tmp = sb("mid_tmp", [P, 2, D], stack=mid)
        mid.close()
        V = sb("V", [P, 2, TT, 512], F32R)
        probT = sb("probT", [P, 2, TT, S], F32R)
        O = sb("O", [P, 2, HG, S], F32R)
        QK = sb("QK", [P, 2, 2, S], F32R)
        hid = [V, probT]

        ps_s = ctx.enter_context(nc.psum_tensor("ps_s", [P, 2, 512], F32))
        ps_c = ctx.enter_context(nc.psum_tensor("ps_c", [P, 2, 512], F32))
        ps_m = ctx.enter_context(nc.psum_tensor("ps_m", [P, 4, 512], F32))
        four = [ps_s[:, 0, :], ps_s[:, 1, :], ps_c[:, 0, :], ps_c[:, 1, :]]

        def f(ap):
            return ap.bitcast(F32)

        x_loaded = [sem(f"x_loaded{b}") for b in range(B)]
        small_loaded = sem("small_loaded")
        rq_loaded = sem("rq_loaded")
        affine_loaded = sem("affine_loaded")
        adab_loaded = sem("adab_loaded")
        wk_loaded = sem("wk_loaded")
        wo_loaded = sem("wo_loaded")
        adaw_loaded = [sem(f"adaw_loaded{n}") for n in range(2)]
        consts = sem("consts")
        const_step = sem("const_step")
        dve_step = sem("dve_step")
        pro_cols = sem("pro_cols")
        pro_condT = sem("pro_condT")
        pro_blocks = sem("pro_blocks")
        pro_blocks_sb = sem("pro_blocks_sb")
        pro_blocksT = sem("pro_blocksT")
        pro_blocksT_sb = sem("pro_blocksT_sb")
        wT_psum = sem("wT_psum")
        wT_sb = sem("wT_sb")
        pro_keys = sem("pro_keys")
        keys_sb = sem("keys_sb")
        keys_sq = sem("keys_sq")
        keys_rms = sem("keys_rms")
        score_col = sem("score_col")
        score_row = sem("score_row")
        score_exp_in = sem("score_exp_in")
        score_exp = sem("score_exp")
        attn_row = sem("attn_row")
        attn_col = sem("attn_col")
        attn_mask = sem("attn_mask")
        att_psum = sem("att_psum")
        att_sb = sem("att_sb")
        proj_psum = sem("proj_psum")
        ada_psum = sem("ada_psum")
        ada_sb = sem("ada_sb")
        adaT_psum = sem("adaT_psum")
        ada_cols_sb = sem("ada_cols_sb")
        ada_stored = sem("ada_stored")
        var_ready = sem("var_ready")
        std_ready = sem("std_ready")
        norm_coef = sem("norm_coef")
        norm_out = sem("norm_out")
        affine_out = sem("affine_out")
        pool_step = sem("pool_step")
        x_new = sem("x_new")
        x_stored = sem("x_stored")
        xT_psum = sem("xT_psum")
        xT_mod = sem("xT_mod")
        xT_split = sem("xT_split")
        xT_stored = [sem(f"xT_stored{n}") for n in range(2)]
        xT_loaded = [sem(f"xT_loaded{n}") for n in range(2)]
        acc_init = sem("acc_init")
        raw_loaded = sem("raw_loaded")
        raw_free = sem("raw_free")
        w_scaled = sem("w_scaled")
        w_hi = sem("w_hi")
        w_split = sem("w_split")
        m_done = sem("m_done")
        m_free = sem("m_free")
        hi_done = sem("hi_done")
        s_done = sem("s_done")
        max_done = sem("max_done")
        exp_done = sem("exp_done")
        inv_done = sem("inv_done")
        norm_done = sem("norm_done")
        c_done = sem("c_done")
        c_hi = sem("c_hi")
        c_lo = sem("c_lo")
        pool_waited = sem("pool_waited")
        sp_waited = sem("sp_waited")
        group_cols_set = sem("group_cols_set")
        gate1_loaded = sem("gate1_loaded")
        xin_loaded = [sem(f"xin_loaded{b}") for b in range(B)]
        mid_x = sem("mid_x")
        mid_xx = sem("mid_xx")
        xx_stored = sem("xx_stored")
        h_done = sem("h_done")
        gelu_done = sem("gelu_done")
        h_hi = sem("h_hi")
        h_lo = sem("h_lo")
        gate2_loaded = sem("gate2_loaded")
        xx_loaded = sem("xx_loaded")
        fin_scaled = sem("fin_scaled")
        fin_done = sem("fin_done")
        out_stored = sem("out_stored")

        def rows(ap, b):
            return ap[b].rearrange("(i p) d -> p i d", p=P)

        w_k = Wk.rearrange("(r p) h -> p r h", p=P)
        w_o = Wo.rearrange("(r p) h -> p r h", p=P)
        ada_v = ada_w.rearrange("(k p) (c n) -> c p k n", p=P, n=512)
        qkv_v = qkv_w.rearrange("(k p) (m g c) -> m g p k c", p=P, m=3, g=G)
        ow_v = out_w.rearrange("(g h p) n -> g p h n", g=G, p=P)
        w1_v = ffn_w1.rearrange("(k p) (g c) -> g p k c", p=P, g=JG)
        w2_v = ffn_w2.rearrange("(g h p) n -> g p h n", g=JG, p=P)

        def bcast(row, parts):
            return row.rearrange("(a n) -> a n", a=1).partition_broadcast(parts)

        def pick(view, g):
            if isinstance(g, int):
                return view[g]
            return view[bass.ds(g, 1)].rearrange("a p k c -> (a p) k c")

        def xT_tile(n):
            return f(xT[:, n].rearrange("p s k t -> p (s k t)"))

        def mod_cols(step):
            return (0, 1) if step < B else (2, 3)

        LOADS1 = B * G // 2

        fin_gate = raw
        FFN_AT = [(MV, MQ), (MK, MO), (MV, MQ), (MK, MO)]

        block = ctx.enter_context(nc.Block())

        @block.sync
        def _(sp):
            sp.dma_start(cond_sb[:, :], cond).then_inc(small_loaded, 16)
            sp.dma_start(bias_rows[0:48, :], qkv_b.rearrange("(r c) -> r c", c=P)).then_inc(small_loaded, 16)
            sp.dma_start(bias_rows[48:64, :], ffn_b1.rearrange("(r c) -> r c", c=P)).then_inc(small_loaded, 16)
            for b in range(B):
                sp.dma_start(acc[:, TT * b:TT * b + TT, :], rows(x, b)).then_inc(x_loaded[b], 16)
            sp.dma_start(Wk_sb[:, :, :], w_k).then_inc(wk_loaded, 16)
            sp.dma_start(Wo_sb[:, :, :], w_o).then_inc(wo_loaded, 16)
            sp.dma_start(prob[0:32, 0, :], bcast(rms_w, 32)).then_inc(rq_loaded, 16)
            sp.dma_start(prob[0:32, 1, :], bcast(cond[1], 32)).then_inc(rq_loaded, 16)
            sp.dma_start(ada[:, :], bcast(ada_b, B)).then_inc(adab_loaded, 16)
            for c in range(6):
                if c >= 2:
                    sp.wait_ge(ada_psum, c - 1)
                sp.dma_start((raw2 if c % 2 == 0 else raw)[:, :, :], ada_v[c]).then_inc(adaw_loaded[c % 2], 16)
            sp.dma_start(affine[:, 0, :], bcast(gamma, P)).then_inc(affine_loaded, 16)
            sp.dma_start(affine[:, 1, :], bcast(beta, P)).then_inc(affine_loaded, 16)
            sp.wait_ge(ada_psum, 6)
            sp.dma_start(raw[:, :, :], pick(qkv_v[MV], 0)).then_inc(raw_loaded, 16)
            sp.wait_ge(ada_sb, 6)
            sp.dma_start(ada_mid, ada[:, :]).then_inc(ada_stored, 16)
            for k, b in enumerate(NORM_ORDER):
                sp.wait_ge(x_new, k + 1)
                sp.dma_start(rows(x_mid, b), acc[:, TT * b:TT * b + TT, :]).then_inc(x_stored, 16)
                sp.wait_ge(xT_split, KT * (k + 1))
                sp.dma_start(xT_mid[0][b], xT_tile(b % 2)).then_inc(xT_stored[b % 2], 16)
                if k < 2:
                    sp.wait_ge(raw_free, k + 1)
                    sp.dma_start(raw[:, :, :], pick(qkv_v[(MQ, MK)[k]], 0)).then_inc(raw_loaded, 16)
            sp.wait_ge(x_stored, 16 * B)
            sp.wait_ge(norm_out, 4 * 2 * B)
            for i in range(B * TT):
                sp.dma_start(acc[:, i, :], bcast(out_b, P)).then_inc(acc_init, 16)

            def load_xT(src, b, wait):
                sp.wait_ge(m_done, wait)
                sp.dma_start(xT_tile(b % 2), src[b]).then_inc(xT_loaded[b % 2], 16)

            def load_raw(src, g, r):
                sp.wait_ge(raw_free, r)
                sp.sem_inc(sp_waited, 1)
                sp.dma_start(raw[:, :, :], pick(src, g)).then_inc(raw_loaded, 16)

            def group(g, last):
                def x_used(b):
                    return NM * g + M_AT[("Q", HG * b + 3)] + 1

                load_raw(ow_v, g, 4 * g + 3)
                load_xT(xT_mid[0], 2, x_used(0))
                load_raw(w1_v if last else qkv_v[MV], 0 if last else g + 1, 4 * g + 4)
                load_xT(xT_mid[0], 3, x_used(1))
                if not last:
                    load_xT(xT_mid[0], 0, x_used(2))
                load_raw(w2_v if last else qkv_v[MQ], 0 if last else g + 1, 4 * g + 5)
                if not last:
                    load_xT(xT_mid[0], 1, x_used(3))
                load_raw(w1_v if last else qkv_v[MK], 1 if last else g + 1, 4 * g + 6)

            sp.wait_ge(xT_stored[0], 32)
            sp.wait_ge(xT_stored[1], 32)
            for n in range(2):
                sp.sem_inc(xT_loaded[n], 16)
            with sp.Fori(0, G - 1) as g:
                group(g, False)
            group(G - 1, True)

            sp.wait_ge(ada_stored, 16)
            sp.wait_ge(m_free, NM * G)
            for b in range(B):
                sp.dma_start(gate1[:, b, :], bcast(ada_mid[b, 2 * D:3 * D], P)).then_inc(gate1_loaded, 16)
            for k, b in enumerate(NORM_ORDER):
                sp.dma_start(x_in[:, TT * b:TT * b + TT, :], rows(x_mid, b)).then_inc(xin_loaded[b], 16)
            load_raw(w2_v, 1, 4 * G + 3)
            for k, b in enumerate(NORM_ORDER):
                sp.wait_ge(mid_xx, TT * (k + 1))
                sp.dma_start(rows(xx_mid, b), x_in[:, TT * b:TT * b + TT, :]).then_inc(xx_stored, 16)
                sp.wait_ge(xT_split, KT * (B + k + 1))
                sp.dma_start(xT_mid[1][b], xT_tile(b % 2)).then_inc(xT_stored[b % 2], 16)
                for i in range(TT):
                    sp.dma_start(acc[:, TT * b + i, :], bcast(ffn_b2, P)).then_inc(acc_init, 16)
            sp.wait_ge(xT_stored[0], 64)
            sp.wait_ge(xT_stored[1], 64)
            for jg in range(JG):
                for b in range(B):
                    i = B * jg + b
                    if i < B * JG - 2:
                        sp.wait_ge(h_done, 4 * (i + 1))
                        sp.dma_start(xT_tile(b % 2), xT_mid[1][(b + 2) % B]).then_inc(xT_loaded[b % 2], 16)
                    if b == 0 and jg < JG - 2:
                        load_raw(w1_v, jg + 2, 4 * G + 4 + 2 * jg)
                    if b == 2 and jg < JG - 2:
                        load_raw(w2_v, jg + 2, 4 * G + 5 + 2 * jg)
            sp.wait_ge(xx_stored, 16 * B)
            for b in range(B):
                sp.wait_ge(fin_done, TT * b)
                if b == 0:
                    sp.wait_ge(m_free, NM * G + 4 * B * JG)
                sp.dma_start(fin_gate[:, b % 2, :], bcast(ada_mid[b, 5 * D:6 * D], P)).then_inc(gate2_loaded, 16)
                sp.dma_start(prob[:, :, :], rows(xx_mid, b)).then_inc(xx_loaded, 16)
                sp.wait_ge(fin_done, TT * (b + 1))
                sp.dma_start(rows(out, b), acc[:, TT * b:TT * b + TT, :]).then_inc(out_stored, 16)
            sp.wait_ge(out_stored, 16 * B)

        def split_piece(mat, q):
            return (lambda t: t[:, :, P * q:P * q + P]) if mat in (MQ, MK) else (lambda t: t[:, q, :])

        @block.gpsimd
        def _(pool):
            step = [0]

            def link(ins):
                step[0] += 1
                ins.then_inc(const_step, 1)
                pool.wait_ge(const_step, step[0])

            link(nc.gpsimd.memset(ident[:, :], 0.0))
            link(nc.gpsimd.affine_select(out=ident[:, :], in_=ident[:, :], compare_op=ALU.not_equal, fill=1.0,
                                         base=0, pattern=[[-1, P]], channel_multiplier=1))
            link(nc.gpsimd.memset(block_ind[:, :], 0.0))
            link(nc.gpsimd.memset(block_ind[0:BLK, 30:31], 1.0))
            link(nc.gpsimd.memset(block_ind[BLK:P, 31:32], 1.0))
            link(nc.gpsimd.memset(batch_mask[:, :], 1.0))
            link(nc.gpsimd.affine_select(out=batch_mask[:, :], in_=batch_mask[:, :], compare_op=ALU.is_ge, fill=0.0,
                                         base=0, pattern=[[-NBLK, B]], channel_multiplier=1))
            link(nc.gpsimd.affine_select(out=batch_mask[:, :], in_=batch_mask[:, :], compare_op=ALU.is_ge, fill=0.0,
                                         base=NBLK - 1, pattern=[[NBLK, B]], channel_multiplier=-1))
            nc.gpsimd.memset(one[:, :], 1.0).then_inc(consts, 1)
            nc.gpsimd.memset(eps[:, :], EPS).then_inc(consts, 1)

            psteps = [0]

            def hold(semaphore, value):
                pool.wait_ge(semaphore, value)
                pool.sem_inc(pool_waited, 1)

            def chain(ins):
                psteps[0] += 1
                ins.then_inc(pool_step, 1)

            def split(mat, dst, q, r, scale):
                at = split_piece(mat, q)
                src, hi, lo = at(raw), at(W[:, dst, HI]), at(W[:, dst, LO])
                if scale != 1.0:
                    nc.gpsimd.tensor_scalar(src, src, scale, 1.0, ALU.mult, ALU.mult).then_inc(w_scaled, 1)
                    hold(w_scaled, r - 1 + q + 1)
                nc.gpsimd.tensor_scalar(hi, src, 1.0, 1.0, ALU.mult, ALU.mult).then_inc(w_hi, 1)
                hold(w_hi, 4 * r + q + 1)
                nc.gpsimd.tensor_tensor(lo, src, f(hi), ALU.subtract).then_inc(w_split, 1)

            def split_matrix(mat, dst, r, scale=1.0, wait=None):
                hold(raw_loaded, 16 * (r + 1))
                for q in range(4):
                    if wait is not None:
                        wait(q)
                    split(mat, dst, q, r, scale)
                hold(w_split, 4 * (r + 1))
                pool.sem_inc(raw_free, 1)

            for k, b in enumerate(NORM_ORDER):
                if k == 0:
                    pool.wait_ge(affine_loaded, 32)
                for i in range(TT):
                    pool.wait_ge(norm_out, 8 * k + i + 1)
                    chain(nc.gpsimd.tensor_tensor(prob[:, i, :], prob[:, i, :], affine[:, 0, :], ALU.mult))
                    pool.wait_ge(pool_step, psteps[0])
                    nc.gpsimd.tensor_tensor(prob[:, i, :], prob[:, i, :], affine[:, 1, :],
                                            ALU.add).then_inc(affine_out, 1)
                if k < 3:
                    mat = (MV, MQ, MK)[k]
                    split_matrix(mat, mat, k, SCALE if mat == MQ else 1.0)

            def normalise(g, n):
                for t in range(TT):
                    hold(inv_done, NS * g + TT * n + t + 1)
                    nc.gpsimd.tensor_scalar(prob[:, t, :], prob[:, t, :], row_inv[:, t:t + 1], 1.0,
                                            ALU.mult, ALU.mult).then_inc(norm_done, 1)

            def group(g, last):
                def used(tile):
                    return lambda q: hold(m_done, NM * g + M_AT[tile] + 1)

                def head_used(q):
                    hold(m_done, NM * g + M_AT[("Q", 12 + q)] + 1)

                normalise(g, 0)
                for n in range(1, SLOTS):
                    if n == 2:
                        split_matrix(MO, MO, 4 * g + 3, 1.0, lambda q: hold(m_done, NM * g + 1))
                    if n == 14:
                        if last:
                            split_matrix(MQ, MV, 4 * g + 4, 1.0, used(("V", 3, 3)))
                        else:
                            split_matrix(MV, MV, 4 * g + 4, 1.0, used(("V", 3, 3)))
                    normalise(g, n)
                if last:
                    split_matrix(MO, MQ, 4 * g + 5, 1.0, lambda q: head_used(3))
                    split_matrix(MQ, MK, 4 * g + 6, 1.0, lambda q: head_used(3))
                else:
                    split_matrix(MQ, MQ, 4 * g + 5, SCALE, head_used)
                    split_matrix(MK, MK, 4 * g + 6, 1.0, head_used)

            with pool.Fori(0, G - 1) as g:
                group(g, False)
            group(G - 1, True)
            split_matrix(MO, MO, 4 * G + 3, 1.0, lambda q: hold(m_done, NM * G))
            for k, b in enumerate(NORM_ORDER):
                for i in range(TT):
                    pool.wait_ge(mid_x, TT * k + i + 1)
                    nc.gpsimd.tensor_tensor(x_in[:, TT * b + i, :], x_in[:, TT * b + i, :], prob[:, i, :],
                                            ALU.add).then_inc(mid_xx, 1)
            for jg in range(2, JG):
                split_matrix(MQ, FFN_AT[jg][0], 4 * G + 4 + 2 * (jg - 2), 1.0,
                             lambda q, jg=jg: hold(h_done, 4 * B * (jg - 1)))
                split_matrix(MO, FFN_AT[jg][1], 4 * G + 5 + 2 * (jg - 2), 1.0,
                             lambda q, jg=jg: hold(m_done, NM * G + 4 * B * (jg - 1)))

        def norm_xT_act(act, step):
            b = NORM_ORDER[step % B]
            c_shift, c_scale = mod_cols(step)
            for k in range(KT):
                n = KT * step + k
                act.wait_ge(xT_psum, n + 1)
                if n >= 2:
                    act.wait_ge(xT_split, n - 1)
                nc.scalar.activation(mod_tmp(step)[:, k % 2, :], four[k], ACT.Identity,
                                     bias=ada_cols[:, c_shift, k, b:b + 1],
                                     scale=ada_cols[:, c_scale, k, b:b + 1]).then_inc(xT_mod, 1)

        def mod_tmp(step):
            return Wo_sb if step < B else mid_tmp

        @block.scalar
        def _(act):
            for m in range(2):
                for k in range(KT):
                    act.wait_ge(wT_psum, KT * m + k + 1)
                    nc.scalar.copy((WkT, WoT)[m][:, k, :], four[k]).then_inc(wT_sb, 1)
            act.wait_ge(keys_sb, 1)
            nc.scalar.activation(prob[0:32, 3, :], prob[0:32, 2, :], ACT.Square,
                                 accum_out=small[:, 0:1]).then_inc(keys_sq, 1)
            act.wait_ge(keys_sq, 1)
            act.wait_ge(consts, 2)
            nc.scalar.activation(small[:, 1:2], small[:, 0:1], ACT.Sqrt, bias=eps[0:32, :],
                                 scale=1.0 / D).then_inc(keys_rms, 1)
            act.wait_ge(score_exp_in, 1)
            nc.scalar.activation(small_row[:, 32:64], small_row[:, 32:64], ACT.Exp).then_inc(score_exp, 1)

            def norm_tiles(call, dst, src):
                act.wait_ge(var_ready, call + 1)
                nc.scalar.activation(std[:, :], mean_var[:, :, 1], ACT.Sqrt, bias=eps[:, :]).then_inc(std_ready, 1)
                act.wait_ge(norm_coef, call + 1)
                for i in range(TT):
                    nc.scalar.activation(dst(i), src(i), ACT.Identity, bias=shift[:, i:i + 1],
                                         scale=rstd[:, i:i + 1]).then_inc(norm_out, 1)

            for k, b in enumerate(NORM_ORDER):
                norm_tiles(2 * k, lambda i: prob[:, i, :], lambda i: prob[:, i, :])
                norm_tiles(2 * k + 1, lambda i: prob[:, i, :], lambda i: acc[:, TT * b + i, :])
                if k == 0:
                    act.wait_ge(ada_cols_sb, 2)
                norm_xT_act(act, k)

            def hi(g, tile, dst, bank, bias):
                act.wait_ge(m_done, NM * g + M_AT[tile] + 1)
                if bias is None:
                    nc.scalar.copy(dst, bank).then_inc(hi_done, 1)
                else:
                    nc.scalar.activation(dst, bank, ACT.Identity, bias=bias).then_inc(hi_done, 1)

            with act.Fori(0, G) as g:
                act.wait_ge(group_cols_set, g + 1)
                for tile in DONE:
                    kind, n = tile[0], tile[1]
                    bank = ps_m[:, M_AT[tile] % 4, :] if tile in M_AT else None
                    if kind == "K":
                        hi(g, tile, QK[:, 1, HI, :], bank, group_cols[:, HG + n % HG:HG + n % HG + 1])
                    elif kind == "Q":
                        hi(g, tile, QK[:, 0, HI, :], bank, group_cols[:, n % HG:n % HG + 1])
                    elif kind == "V":
                        hi(g, tile, V[:, HI, tile[2], :], bank, None)
                    elif kind == "O":
                        hi(g, tile, O[:, HI, n % HG, :], bank, group_cols[:, 2 * HG + n % HG:2 * HG + n % HG + 1])
                    elif kind == "S":
                        t = tile[2]
                        act.wait_ge(max_done, NS * g + TT * n + t + 1)
                        nc.scalar.activation(prob[:, t, :], ps_s[:, (TT * n + t) % 2, :], ACT.Exp,
                                             bias=neg_max[:, t:t + 1],
                                             accum_out=row_sum[:, t:t + 1]).then_inc(exp_done, 1)
                    elif kind == "C":
                        j = tile[2]
                        act.wait_ge(c_done, NS * g + TT * n + j + 1)
                        nc.scalar.copy(probT[:, HI, j, :], ps_c[:, (TT * n + j) % 2, :]).then_inc(c_hi, 1)

            for k, b in enumerate(NORM_ORDER):
                norm_tiles(2 * B + k, lambda i: acc[:, TT * b + i, :], lambda i: prob[:, i, :])
                norm_xT_act(act, B + k)

            act.wait_ge(mid_xx, B * TT)
            with act.Fori(0, JG // 2) as it:
                act.wait_ge(group_cols_set, G + it + 1)
                for u in range(2 * B):
                    for j in range(4):
                        n = 4 * u + j
                        act.wait_ge(h_done, 8 * B * it + n + 1)
                        if n >= 4:
                            act.wait_ge(h_lo, 8 * B * it + n - 3)
                        col = 4 * (u // B) + j
                        nc.scalar.activation(prob[:, j, :], four[j], ACT.Gelu,
                                             bias=group_cols[:, col:col + 1]).then_inc(gelu_done, 1)
                act.wait_ge(h_lo, 8 * B * (it + 1))

        @block.vector
        def _(dve):
            count = [0]

            def link(ins):
                count[0] += 1
                ins.then_inc(dve_step, 1)
                dve.wait_ge(dve_step, count[0])

            v = nc.vector
            dve.wait_ge(pro_cols, 1)
            link(v.tensor_copy(cols[:, :], ps_m[:, 0, 0:64]))
            link(v.tensor_scalar(cols[:, 0:H], cols[:, 0:H], SCALE, None, ALU.mult))
            v.tensor_copy(condT[:, :, :], ps_m[:, 1, 0:16].rearrange("p (k b) -> p k b", b=B)).then_inc(pro_condT, 1)
            dve.wait_ge(pro_blocks, 1)
            v.tensor_copy(blocks[:, :], ps_m[0:32, 2, :]).then_inc(pro_blocks_sb, 1)
            dve.wait_ge(pro_blocksT, 1)
            v.tensor_copy(blocksT[:, :, :], ps_m[:, 3, 0:128].rearrange("p (k n) -> p k n", n=32)) \
                .then_inc(pro_blocksT_sb, 1)
            dve.wait_ge(rq_loaded, 32)
            link(v.tensor_tensor(prob[0:32, 1, :], prob[0:32, 1, :], prob[0:32, 0, :], ALU.mult))
            dve.wait_ge(pro_keys, 1)
            v.tensor_copy(prob[0:32, 2, :], ps_m[0:32, 0, :]).then_inc(keys_sb, 1)
            dve.wait_ge(keys_sb, 1)
            link(v.tensor_tensor(prob[0:32, 0, :], prob[0:32, 1, :], prob[0:32, 2, :], ALU.mult))
            link(v.reduce_sum(small[:, 2:3], prob[0:32, 0, :], axis=AX_X))
            dve.wait_ge(keys_rms, 1)
            link(v.reciprocal(small[:, 3:4], small[:, 1:2]))
            v.tensor_tensor(small[:, 4:5], small[:, 2:3], small[:, 3:4], ALU.mult).then_inc(score_col, 1)
            dve.wait_ge(score_row, 1)
            r = small_row
            scores = ps_m[0:1, 1, 64:96].rearrange("p (b n) -> p b n", n=NBLK)
            expd = r[:, 32:64].rearrange("p (b n) -> p b n", n=NBLK)
            link(v.tensor_reduce(r[:, 0:4], scores, axis=AX_X, op=ALU.max))
            v.tensor_tensor(expd, scores, r[:, 0:4].unsqueeze(2).to_broadcast([1, B, NBLK]),
                            ALU.subtract).then_inc(score_exp_in, 1)
            dve.wait_ge(score_exp, 1)
            link(v.reduce_sum(r[:, 4:8], expd, axis=AX_X))
            link(v.reciprocal(r[:, 8:12], r[:, 4:8]))
            v.tensor_tensor(r[:, 64:96].rearrange("p (b n) -> p b n", n=NBLK), expd,
                            r[:, 8:12].unsqueeze(2).to_broadcast([1, B, NBLK]), ALU.mult).then_inc(attn_row, 1)
            dve.wait_ge(attn_col, 1)
            link(v.tensor_copy(small[:, 5:6], ps_m[0:32, 1, 100:101]))
            dve.wait_ge(consts, 2)
            v.tensor_scalar(small[:, 8:12], batch_mask[:, :], small[:, 5:6], None, ALU.mult).then_inc(attn_mask, 1)
            dve.wait_ge(att_psum, 1)
            dve.wait_ge(wT_psum, KT)
            att = ps_m[:, 1, 128:144]
            for k in range(KT):
                last = v.tensor_copy(att_bc[:, k], att[:, B * k:B * k + B].unsqueeze(2).to_broadcast([P, B, P]))
                if k < KT - 1:
                    link(last)
            last.then_inc(att_sb, 1)
            dve.wait_ge(adab_loaded, 16)
            for c in range(6):
                dve.wait_ge(ada_psum, c + 1)
                v.tensor_tensor(ada[:, 512 * c:512 * c + 512], ada[:, 512 * c:512 * c + 512],
                                four[c % 2][0:B, :], ALU.add).then_inc(ada_sb, 1)
            dve.wait_ge(adaT_psum, 1)
            v.tensor_copy(ada_cols[:, :, :, :], ps_c[:, 0, 0:64].rearrange("p (y k b) -> p y k b", y=4, k=KT)) \
                .then_inc(ada_cols_sb, 1)
            dve.wait_ge(ada_cols_sb, 1)
            for y in (1, 3):
                last = v.tensor_scalar(ada_cols[:, y], ada_cols[:, y], 1.0, None, ALU.add)
                if y == 1:
                    link(last)
            last.then_inc(ada_cols_sb, 1)

            def coefficients(call):
                dve.wait_ge(std_ready, call + 1)
                link(v.reciprocal(rstd[:, :], std[:, :]))
                v.scalar_tensor_tensor(out=shift[:, :], in0=mean_var[:, :, 0], scalar=-1.0, in1=rstd[:, :],
                                       op0=ALU.mult, op1=ALU.mult).then_inc(norm_coef, 1)

            def moments(src):
                for i in range(TT):
                    link(v.bn_stats(stats[:, i, :], src(i)))
                    last = v.bn_aggr(mean_var[:, i, :], stats[:, i, :])
                    if i < TT - 1:
                        link(last)
                last.then_inc(var_ready, 1)

            def split_xT(step):
                b = NORM_ORDER[step % B]
                if step % B >= 2 or step >= B:
                    dve.wait_ge(xT_stored[b % 2], 16 * (step // 2))
                for k in range(KT):
                    dve.wait_ge(xT_mod, KT * step + k + 1)
                    tmp = mod_tmp(step)[:, k % 2, :]
                    link(v.tensor_copy(xT[:, b % 2, HI, k, :], tmp))
                    v.tensor_tensor(xT[:, b % 2, LO, k, :], tmp, f(xT[:, b % 2, HI, k, :]),
                                    ALU.subtract).then_inc(xT_split, 1)

            for k, b in enumerate(NORM_ORDER):
                dve.wait_ge(proj_psum, B)
                if k:
                    dve.wait_ge(xT_psum, KT * k)
                for i in range(TT):
                    link(v.tensor_tensor(prob[:, i, :], acc[:, TT * b + i, :], ps_m[:, b, :], ALU.add))
                moments(lambda i: prob[:, i, :])
                coefficients(2 * k)
                for i in range(TT):
                    dve.wait_ge(affine_out, TT * k + i + 1)
                    link(v.tensor_tensor(acc[:, TT * b + i, :], acc[:, TT * b + i, :], prob[:, i, :], ALU.add))
                dve.sem_inc(x_new, 1)
                moments(lambda i: acc[:, TT * b + i, :])
                coefficients(2 * k + 1)
                split_xT(k)

            def take(g, tile):
                if tile in SPLIT_AT:
                    dve.wait_ge(hi_done, NSPLIT * g + SPLIT_AT[tile] + 1)
                else:
                    dve.wait_ge(m_done, NM * g + M_AT[tile] + 1)

            def lo(g, tile, dst, hi_part, bank, bias):
                take(g, tile)
                if bias is None:
                    v.tensor_tensor(dst, bank, f(hi_part), ALU.subtract).then_inc(m_free, 1)
                else:
                    v.scalar_tensor_tensor(out=dst, in0=bank, scalar=bias, in1=f(hi_part), op0=ALU.add,
                                           op1=ALU.subtract).then_inc(m_free, 1)

            def inverse(g, s):
                dve.wait_ge(exp_done, NS * g + s + 1)
                v.reciprocal(row_inv[:, s % TT:s % TT + 1], row_sum[:, s % TT:s % TT + 1]).then_inc(inv_done, 1)

            dve.wait_ge(acc_init, 16 * B * TT)
            with dve.Fori(0, G) as g:
                v.tensor_copy(group_cols[:, :].rearrange("p (m h) -> p m h", m=3),
                              cols[:, 0:3 * H].rearrange("p (m h) -> p m h", m=3)[:, :, bass.ds(HG * g, HG)]) \
                    .then_inc(group_cols_set, 1)
                dve.wait_ge(group_cols_set, g + 1)
                for tile in DONE:
                    kind, n = tile[0], tile[1]
                    bank = ps_m[:, M_AT[tile] % 4, :] if tile in M_AT else None
                    if kind == "K":
                        lo(g, tile, QK[:, 1, LO, :], QK[:, 1, HI, :], bank, group_cols[:, HG + n % HG:HG + n % HG + 1])
                    elif kind == "Q":
                        lo(g, tile, QK[:, 0, LO, :], QK[:, 0, HI, :], bank, group_cols[:, n % HG:n % HG + 1])
                    elif kind == "V":
                        lo(g, tile, V[:, LO, tile[2], :], V[:, HI, tile[2], :], bank, None)
                    elif kind == "O":
                        lo(g, tile, O[:, LO, n % HG, :], O[:, HI, n % HG, :], bank,
                           group_cols[:, 2 * HG + n % HG:2 * HG + n % HG + 1])
                    elif kind == "Y":
                        take(g, tile)
                        at = TT * n + tile[2]
                        v.tensor_tensor(acc[:, at, :], acc[:, at, :], bank, ALU.add).then_inc(m_free, 1)
                    elif kind == "S":
                        s = TT * n + tile[2]
                        dve.wait_ge(s_done, NS * g + s + 1)
                        v.tensor_reduce(neg_max[:, s % TT:s % TT + 1], ps_s[:, s % 2, :], axis=AX_X, op=ALU.max,
                                        negate=True).then_inc(max_done, 1)
                        if tile[2] >= 1:
                            inverse(g, s - 1)
                        if tile[2] == TT - 1:
                            inverse(g, s)
                    elif kind == "C":
                        j = tile[2]
                        dve.wait_ge(c_hi, NS * g + TT * n + j + 1)
                        v.tensor_tensor(probT[:, LO, j, :], ps_c[:, (TT * n + j) % 2, :], f(probT[:, HI, j, :]),
                                        ALU.subtract).then_inc(c_lo, 1)

            dve.wait_ge(gate1_loaded, 16 * B)
            for k, b in enumerate(NORM_ORDER):
                dve.wait_ge(xin_loaded[b], 16)
                if k:
                    dve.wait_ge(norm_out, 8 * B + TT * k)
                    dve.wait_ge(mid_xx, TT * k)
                for i in range(TT):
                    link(v.tensor_tensor(prob[:, i, :], acc[:, TT * b + i, :], gate1[:, b, :], ALU.mult))
                    link(v.tensor_tensor(prob[:, i, :], prob[:, i, :], x_in[:, TT * b + i, :], ALU.add))
                    dve.sem_inc(mid_x, 1)
                moments(lambda i: prob[:, i, :])
                coefficients(2 * B + k)
                split_xT(B + k)

            dve.wait_ge(acc_init, 2 * 16 * B * TT)
            dve.wait_ge(xx_stored, 16 * B)
            with dve.Fori(0, JG // 2) as it:
                v.tensor_copy(group_cols[:, 0:8], cols[:, bass.ds(3 * H + 8 * it, 8)]).then_inc(group_cols_set, 1)
                def split_hidden(u):
                    for j in range(4):
                        n = 4 * u + j
                        dve.wait_ge(gelu_done, 8 * B * it + n + 1)
                        v.tensor_copy(hid[u % 2][:, HI, j, :], prob[:, j, :]).then_inc(h_hi, 1)
                        dve.wait_ge(h_hi, 8 * B * it + n + 1)
                        v.tensor_tensor(hid[u % 2][:, LO, j, :], prob[:, j, :], f(hid[u % 2][:, HI, j, :]),
                                        ALU.subtract).then_inc(h_lo, 1)

                split_hidden(0)
                for u in range(2 * B):
                    if u < 2 * B - 1:
                        split_hidden(u + 1)
                    for i in range(TT):
                        at = TT * (u % B) + i
                        dve.wait_ge(m_done, NM * G + 8 * B * it + 4 * u + i + 1)
                        v.tensor_tensor(acc[:, at, :], acc[:, at, :], ps_m[:, i, :], ALU.add).then_inc(m_free, 1)

            for b in range(B):
                dve.wait_ge(gate2_loaded, 16 * (b + 1))
                dve.wait_ge(xx_loaded, 16 * (b + 1))
                for i in range(TT):
                    at = TT * b + i
                    v.tensor_tensor(acc[:, at, :], acc[:, at, :], fin_gate[:, b % 2, :], ALU.mult) \
                        .then_inc(fin_scaled, 1)
                    dve.wait_ge(fin_scaled, at + 1)
                    v.tensor_tensor(acc[:, at, :], acc[:, at, :], prob[:, i, :], ALU.add).then_inc(fin_done, 1)

        @block.tensor
        def _(pe):
            mm, tr = nc.tensor.matmul, nc.tensor.transpose
            pe.wait_ge(consts, 2)
            pe.wait_ge(small_loaded, 48)
            tr(ps_m[:, 0, 0:64], bias_rows[:, :], ident[0:64, 0:64])
            for k in range(KT):
                last = tr(ps_m[:, 1, B * k:B * k + B], cond_sb[:, P * k:P * k + P], ident[0:B, 0:B])
            last.then_inc(pro_cols, 1)
            for b in range(B):
                pe.wait_ge(x_loaded[b], 16)
                for i in range(TT):
                    n = TT * b + i
                    last = mm(ps_m[0:32, 2, :], block_ind[:, 30 - 2 * n:62 - 2 * n], acc[:, n, :],
                              start=(n == 0), stop=(n == B * TT - 1))
            last.then_inc(pro_blocks, 1)
            for m in range(2):
                pe.wait_ge((wk_loaded, wo_loaded)[m], 16)
                for k in range(KT):
                    if m:
                        pe.wait_ge(wT_sb, k + 1)
                    for r in range(KT):
                        last = tr(four[k][:, P * r:P * r + P], (Wk_sb, Wo_sb)[m][:, r, P * k:P * k + P], ident[:, :])
                    last.then_inc(wT_psum, 1)
            pe.wait_ge(pro_blocks_sb, 1)
            for k in range(KT):
                last = tr(ps_m[:, 3, 32 * k:32 * k + 32], blocks[:, P * k:P * k + P], ident[0:32, 0:32])
            last.then_inc(pro_blocksT, 1)
            pe.wait_ge(pro_blocksT_sb, 1)
            pe.wait_ge(pro_condT, 1)
            pe.wait_ge(wT_sb, KT)
            for k in range(KT):
                last = mm(ps_m[0:32, 0, :], blocksT[:, k, :], WkT[:, k, :], start=(k == 0), stop=(k == KT - 1))
            last.then_inc(pro_keys, 1)
            pe.wait_ge(score_col, 1)
            tr(ps_m[0:1, 1, 64:96], small[:, 4:5], ident[0:32, 0:32]).then_inc(score_row, 1)
            pe.wait_ge(attn_row, 1)
            mm(ps_m[0:32, 1, 100:101], small_row[:, 64:96], one[:, :], start=True, stop=True).then_inc(attn_col, 1)
            pe.wait_ge(attn_mask, 1)
            for k in range(KT):
                last = mm(ps_m[:, 1, 128 + B * k:128 + B * k + B], blocks[:, P * k:P * k + P], small[:, 8:12],
                          start=True, stop=True)
            last.then_inc(att_psum, 1)
            pe.wait_ge(att_sb, 1)
            pe.wait_ge(wT_sb, 2 * KT)
            for b in range(B):
                for k in range(KT):
                    last = mm(ps_m[:, b, :], att_bc[:, k, b, :], WoT[:, k, :], start=(k == 0), stop=(k == KT - 1))
                last.then_inc(proj_psum, 1)
            for c in range(6):
                pe.wait_ge(adaw_loaded[c % 2], 16 * (c // 2 + 1))
                if c >= 2:
                    pe.wait_ge(ada_sb, c - 1)
                for k in range(KT):
                    last = mm(four[c % 2][0:B, :], condT[:, k, :], (raw2 if c % 2 == 0 else raw)[:, k, :],
                              start=(k == 0), stop=(k == KT - 1))
                last.then_inc(ada_psum, 1)
            pe.wait_ge(ada_sb, 6)
            for y, part in enumerate((0, 1, 3, 4)):
                for k in range(KT):
                    at = 16 * y + B * k
                    last = tr(ps_c[:, 0, at:at + B], ada[:, 512 * part + P * k:512 * part + P * k + P],
                              ident[0:B, 0:B])
            last.then_inc(adaT_psum, 1)

            def transpose_norm(step, src):
                pe.wait_ge(norm_out, norm_outs(step))
                for k in range(KT):
                    if step:
                        pe.wait_ge(xT_mod, KT * (step - 1) + k + 1)
                    elif k == 2:
                        pe.wait_ge(ada_cols_sb, 2)
                    for i in range(TT):
                        last = tr(four[k][:, P * i:P * i + P], src(i)[:, P * k:P * k + P], ident[:, :])
                    last.then_inc(xT_psum, 1)

            def norm_outs(step):
                return 8 * (step + 1) if step < B else 8 * B + TT * (step - B + 1)

            for k, b in enumerate(NORM_ORDER):
                transpose_norm(k, lambda i: prob[:, i, :])

            def product(out_ap, stationary, moving, k0, k1, last_k):
                for k in range(k0, k1):
                    for n, (a, c) in enumerate(PAIRS):
                        last = mm(out_ap, stationary(a, k), moving(c, k), start=(k == 0 and n == 0),
                                  stop=(k == last_k - 1 and n == len(PAIRS) - 1))
                return last

            with pe.Fori(0, G) as g:
                for s in ORDER:
                    kind, n = s[0], s[1]
                    b, h = n // HG, n % HG
                    xb = xT[:, (b if kind in "KQ" else n) % 2]
                    tile = ("O", n) if kind == "D" else (s[0], s[1]) if kind in "KQ" else s
                    if tile in M_AT:
                        m = M_AT[tile]
                        bank = ps_m[:, m % 4, :]
                        first = s[2] == 0 if kind in "KQD" else True
                        if first and m >= 4:
                            pe.wait_ge(m_free, NM * g + m - 3)
                    if kind in "KQ":
                        if s[2] == 0 and h == 0 and kind == "K":
                            pe.wait_ge(xT_split, KT * B)
                            pe.wait_ge(xT_loaded[b % 2], 16 * (2 * g + b // 2 + 1))
                        if s[2] == 0 and b == 0 and kind == "K":
                            pe.wait_ge(w_split, 16 * g + 8 + h + 1)
                        mat = MK if kind == "K" else MQ
                        last = product(bank, lambda a, k: W[:, mat, a, k, P * h:P * h + P],
                                       lambda c, k: xb[:, c, k, :], s[2], s[3], KT)
                        if s[3] == KT:
                            last.then_inc(m_done, 1)
                    elif kind == "V":
                        j = s[2]
                        if n == 0 and j == 0:
                            pe.wait_ge(w_split, 16 * g + 4)
                        product(bank, lambda a, k: xb[:, a, k, P * j:P * j + P],
                                lambda c, k: W[:, MV, c, k, :], 0, KT, KT).then_inc(m_done, 1)
                    elif kind == "Y":
                        i = s[2]
                        if i == 0:
                            pe.wait_ge(w_split, 16 * g + 16)
                            pe.wait_ge(m_free, NM * g + M_AT[("O", HG * n + 3)] + 1)
                        product(bank, lambda a, k: O[:, a, k, P * i:P * i + P],
                                lambda c, k: W[:, MO, c, k, :], 0, HG, HG).then_inc(m_done, 1)
                    elif kind == "S":
                        t = s[2]
                        if t == 0:
                            pe.wait_ge(m_free, NM * g + M_AT[("Q", n)] + 1)
                        if TT * n + t >= 2:
                            pe.wait_ge(exp_done, NS * g + TT * n + t - 1)
                        product(ps_s[:, (TT * n + t) % 2, :], lambda a, k: QK[:, 0, a, P * t:P * t + P],
                                lambda c, k: QK[:, 1, c, :], 0, 1, 1).then_inc(s_done, 1)
                    elif kind == "C":
                        j = s[2]
                        if j == 0:
                            pe.wait_ge(norm_done, NS * g + TT * n + TT)
                        if TT * n + j >= 2:
                            pe.wait_ge(c_lo, NS * g + TT * n + j - 1)
                        for t in range(TT):
                            last = tr(ps_c[:, (TT * n + j) % 2, P * t:P * t + P], prob[:, t, P * j:P * j + P],
                                      ident[:, :])
                        last.then_inc(c_done, 1)
                    elif kind == "D":
                        j = s[2]
                        if j == 0 and h == 0:
                            pe.wait_ge(m_free, NM * g + M_AT[("V", b, TT - 1)] + 1)
                        pe.wait_ge(c_lo, NS * g + TT * n + j + 1)
                        last = product(bank, lambda a, k: V[:, a, k, P * h:P * h + P],
                                       lambda c, k: probT[:, c, k, :], j, j + 1, TT)
                        if j == TT - 1:
                            last.then_inc(m_done, 1)
                pe.wait_ge(m_free, NM * g + NM)

            for k, b in enumerate(NORM_ORDER):
                transpose_norm(B + k, lambda i: acc[:, TT * b + i, :])

            pe.wait_ge(xT_split, 2 * KT * B)
            with pe.Fori(0, JG // 2) as it:
                def hidden(u):
                    b, jl = u % B, u // B
                    w1 = FFN_AT[jl][0]
                    pe.wait_ge(xT_loaded[b % 2], 16 * (LOADS1 + 4 * it + u // 2))
                    for j in range(4):
                        n = 4 * u + j
                        if b == 0:
                            pe.wait_ge(w_split, 16 * G + 16 * it + 8 * jl + j + 1)
                        if n >= 4:
                            pe.wait_ge(gelu_done, 8 * B * it + n - 3)
                        product(four[j], lambda a, k: W[:, w1, a, k, P * j:P * j + P],
                                lambda c, k: xT[:, b % 2, c, k, :], 0, KT, KT).then_inc(h_done, 1)

                hidden(0)
                for u in range(2 * B):
                    if u < 2 * B - 1:
                        hidden(u + 1)
                    b, jl = u % B, u // B
                    w2 = FFN_AT[jl][1]
                    pe.wait_ge(h_lo, 8 * B * it + 4 * u + 4)
                    if b == 0:
                        pe.wait_ge(w_split, 16 * G + 16 * it + 8 * jl + 8)
                    for i in range(TT):
                        if u:
                            pe.wait_ge(m_free, NM * G + 8 * B * it + 4 * (u - 1) + i + 1)
                        product(ps_m[:, i, :], lambda a, k: hid[u % 2][:, a, k, P * i:P * i + P],
                                lambda c, k: W[:, w2, c, k, :], 0, 4, 4).then_inc(m_done, 1)
                pe.wait_ge(m_free, NM * G + 8 * B * (it + 1))


_INS = ["x", "cond_2048", "L0_cond_rms_weight", "L0_cond_Wk", "L0_cond_Wo", "L0_cond_ln_gamma", "L0_cond_ln_beta",
        "L1_cond_ada_w", "L1_cond_ada_b", "L1_cond_qkv_w", "L1_cond_qkv_b", "L1_cond_out_w", "L1_cond_out_b",
        "L1_cond_ffn_w1", "L1_cond_ffn_b1", "L1_cond_ffn_w2", "L1_cond_ffn_b2"]


def kernel(**inputs):
    import numpy as _np
    import concourse.bacc as _bacc
    from concourse import mybir as _mybir
    from concourse.bass_utils import run_bass_kernel_spmd as _run

    nc = _bacc.Bacc("TRN2", target_bir_lowering=False, num_devices=1)
    arrays, args = {}, []
    for name in _INS:
        a = _np.ascontiguousarray(inputs[name])
        arrays[f"in_{name}"] = a
        args.append(nc.dram_tensor(f"in_{name}", a.shape, _mybir.dt.from_np(a.dtype), kind="ExternalInput").ap())
    out = nc.dram_tensor("out_0", (B, S, D), F32, kind="ExternalOutput").ap()
    build(nc, *args, out)
    r = _run(nc, [arrays], core_ids=[0])
    return r.results[0]["out_0"]
```

```python
from contextlib import ExitStack

import concourse.bass as bass
from concourse import mybir

F32 = mybir.dt.float32
F32R = mybir.dt.float32r
ACT = mybir.ActivationFunctionType
ALU = mybir.AluOpType
AX_X = mybir.AxisListType.X

P = 128
B = 4
S = 512
D = 512
KT = D // P
TT = S // P
H = 16
DH = 128
HG = 4
G = H // HG
MLP = 2048
JG = MLP // 512
NBLK = 8
BLK = S // NBLK
SCALE = float(DH) ** -0.5
EPS = 1e-6
HI, LO = 0, 1
MQ, MK, MV, MO = 0, 1, 2, 3
PAIRS = ((HI, HI), (HI, LO), (LO, HI))
SLOTS = B * HG


def group_order(first, last):
    steps = [("X", 0, k) for k in range(KT)] if first else []
    steps += [("K", 0, 0, KT), ("Q", 0, 0, KT)] + [("V", 0, j) for j in range(TT)]
    steps += [("S", 0, t) for t in range(TT)]
    for n in range(SLOTS):
        b, more = n // HG, n < SLOTS - 1
        if more:
            steps += [("K", n + 1, 0, 4), ("C", n, 0), ("Q", n + 1, 0, 2), ("C", n, 1),
                      ("Q", n + 1, 2, 4), ("C", n, 2), ("C", n, 3)]
        else:
            steps += [("C", n, j) for j in range(TT)]
        if n % HG == 0 and n:
            steps += [("V", b, j) for j in range(TT)] + [("Y", b - 1, i) for i in range(TT)]
        if first and n % HG == 2 and b < B - 1:
            steps += [("X", b + 1, k) for k in range(KT)]
        if last and n >= SLOTS - 2:
            steps += [("X", n - SLOTS + 2, k) for k in range(KT)]
        if more:
            steps += [("D", n, 0), ("S", n + 1, 0), ("S", n + 1, 1), ("D", n, 1), ("D", n, 2),
                      ("S", n + 1, 2), ("S", n + 1, 3), ("D", n, 3)]
        else:
            steps += [("D", n, j) for j in range(TT)]
    return steps + [("Y", B - 1, i) for i in range(TT)]


def mlp_order():
    steps = [("H", 0, j) for j in range(4)]
    for u in range(B * JG):
        if u + 1 in (2, 3):
            steps += [("X", u + 1, k) for k in range(KT)]
        if u + 1 < B * JG:
            steps += [("H", u + 1, j) for j in range(4)]
        steps += [("Z", u, i) for i in range(TT)]
    return steps


def after(tiles, extra):
    out = []
    for t in tiles:
        out.append(t)
        out += extra.get(t, [])
    assert len(out) == len(tiles) + sum(map(len, extra.values()))
    return out


class Plan:

    def __init__(self, order):
        self.order = order
        self.done = []
        for s in order:
            if s[0] in "KQ":
                if s[3] == KT:
                    self.done.append((s[0], s[1]))
            elif s[0] == "D":
                if s[2] == TT - 1:
                    self.done.append(("O", s[1]))
            else:
                self.done.append(s)
        m_tiles = [t for t in self.done if t[0] in "XKQVOYZ"]
        self.at = {t: n for n, t in enumerate(m_tiles)}
        self.tiles = len(m_tiles)
        self.hi_at = {t: n for n, t in enumerate(t for t in m_tiles if t[0] not in "YZ")}
        self.his = len(self.hi_at)
        assert self.tiles % 4 == 0


FIRST, MIDDLE, LAST, MLP_PLAN = (Plan(group_order(True, False)), Plan(group_order(False, False)),
                                 Plan(group_order(False, True)), Plan(mlp_order()))
NS = SLOTS * TT


def plan_of(g):
    return MIDDLE if not isinstance(g, int) else FIRST if g == 0 else LAST if g == G - 1 else MIDDLE


def m_base(g):
    return 0 if isinstance(g, int) and g == 0 else MIDDLE.tiles * g + (FIRST.tiles - MIDDLE.tiles)


def hi_base(g):
    return 0 if isinstance(g, int) and g == 0 else MIDDLE.his * g + (FIRST.his - MIDDLE.his)


M_MLP = m_base(G - 1) + LAST.tiles
HI_MLP = hi_base(G - 1) + LAST.his

FIRST_EXTRA = {}
for _b in range(1, B):
    _p = _b - 1
    for _i in range(TT):
        FIRST_EXTRA[("V", _p, _i)] = [("sum", _b, _i)]
    if _p == 0:
        FIRST_EXTRA[("K", 1)] = [("aff", _b, 0)]
        FIRST_EXTRA[("Q", 1)] = [("aff", _b, 1)]
        FIRST_EXTRA[("O", 0)] = [("aff", _b, 2)]
        FIRST_EXTRA[("K", 2)] = [("aff", _b, 3)]
        FIRST_EXTRA[("O", 1)] = [("hat", _b, 0), ("hat", _b, 1)]
        FIRST_EXTRA[("K", 3)] = [("hat", _b, 2), ("hat", _b, 3)]
    else:
        for _i in range(TT):
            FIRST_EXTRA[("Y", _p - 1, _i)] = [("aff", _b, _i)]
        FIRST_EXTRA[("K", HG * _p + 2)] = [("hat", _b, 0), ("hat", _b, 1)]
        FIRST_EXTRA[("K", HG * _p + 3)] = [("hat", _b, 2), ("hat", _b, 3)]
LAST_EXTRA = {}
for _b in range(2):
    _n = HG * (_b + 1)
    LAST_EXTRA[("O", _n)] = [("res", _b, 0)]
    LAST_EXTRA[("K", _n + 2)] = [("res", _b, 1)]
    LAST_EXTRA[("O", _n + 1)] = [("res", _b, 2)]
    LAST_EXTRA[("K", _n + 3)] = [("res", _b, 3)]
    LAST_EXTRA[("O", _n + 2)] = [("hat", _b, 0), ("hat", _b, 1)]
    LAST_EXTRA[("K", _n + 4)] = [("hat", _b, 2), ("hat", _b, 3)]
MLP_EXTRA = {}
for _b in (2, 3):
    for _i in range(TT):
        MLP_EXTRA[("H", _b - 1, _i)] = [("res", _b, _i)]
        MLP_EXTRA[("Z", _b - 2, _i)] = [("hat", _b, _i)]


def build(nc, x, cond, rms_w, Wk, Wo, gamma, beta, ada_w, ada_b, qkv_w, qkv_b, out_w, out_b,
          ffn_w1, ffn_b1, ffn_w2, ffn_b2, out):
    ctx = ExitStack()
    with ctx:
        def sb(name, shape, dt=F32, stack=ctx):
            return stack.enter_context(nc.sbuf_tensor(name, shape, dt))

        def sem(name):
            return ctx.enter_context(nc.semaphore(name))

        x_mid = nc.dram_tensor("x_mid", (B, S, D), F32, kind="Internal").ap()
        xx_mid = nc.dram_tensor("xx_mid", (B, S, D), F32, kind="Internal").ap()
        xT_mid = [nc.dram_tensor(f"xT_mid{n}", (B, P, 2 * KT * S), F32, kind="Internal").ap() for n in range(2)]
        proj_mid = nc.dram_tensor("proj_mid", (B, D), F32, kind="Internal").ap()
        ada_mid = nc.dram_tensor("ada_mid", (B, 6 * D), F32, kind="Internal").ap()

        acc = sb("acc", [P, B * TT, D])
        W = sb("W", [P, 4, 2, 4, 512], F32R)
        raw = sb("raw", [P, 4, 512])
        prob = sb("prob", [P, TT, S])
        wide = sb("wide", [P, 2, D])
        proj = sb("proj", [P, D])
        ident = sb("ident", [P, P])
        cols = sb("cols", [P, 64])
        group_cols = sb("group_cols", [P, 12])
        ada_cols = sb("ada_cols", [P, 4, KT, B])
        neg_max = sb("neg_max", [P, TT])
        row_sum = sb("row_sum", [P, TT])
        row_inv = sb("row_inv", [P, TT])
        stats = sb("stats", [P, TT, 6])
        mean_var = sb("mean_var", [P, TT, 2])
        rstd = sb("rstd", [P, TT])
        minus_half = sb("minus_half", [P, TT])

        start = ExitStack()
        ada_raw = sb("ada_raw", [P, 4, KT, 512], stack=start)
        start.close()
        xT = sb("xT", [P, 2, 2, KT, S], F32R)
        start = ExitStack()
        WkT = sb("WkT", [P, KT, D], stack=start)
        WoT = sb("WoT", [P, KT, D], stack=start)
        Wk_sb = sb("Wk_sb", [P, KT, D], stack=start)
        Wo_sb = sb("Wo_sb", [P, KT, D], stack=start)
        raw2 = sb("raw2", [P, 4, 512], stack=start)
        ada = sb("ada", [B, 6 * D], stack=start)
        blocks = sb("blocks", [32, D], stack=start)
        blocksT = sb("blocksT", [P, KT, 32], stack=start)
        bias_rows = sb("bias_rows", [64, P], stack=start)
        small_row = sb("small_row", [1, 96], stack=start)
        block_ind = sb("block_ind", [P, 62], stack=start)
        batch_mask = sb("batch_mask", [32, B], stack=start)
        one = sb("one", [1, 1], stack=start)
        condT = sb("condT", [P, KT, B], stack=start)
        small = sb("small", [32, 16], stack=start)
        start.close()
        att_bc = Wk_sb[:, :, :].rearrange("p k (b c) -> p k b c", b=B)
        V = sb("V", [P, 2, TT, 512], F32R)
        probT = sb("probT", [P, 2, TT, S], F32R)
        later = ExitStack()
        O = sb("O", [P, 2, HG, S], F32R, stack=later)
        later.close()
        xx_in = sb("xx_in", [P, 2, TT, D])
        QK = sb("QK", [P, 2, 2, S], F32R)
        hid = [V, probT]
        cond_sb = proj[0:B, :]

        ps_s = ctx.enter_context(nc.psum_tensor("ps_s", [P, 2, 512], F32))
        ps_c = ctx.enter_context(nc.psum_tensor("ps_c", [P, 2, 512], F32))
        ps_m = ctx.enter_context(nc.psum_tensor("ps_m", [P, 4, 512], F32))
        four = [ps_s[:, 0, :], ps_s[:, 1, :], ps_c[:, 0, :], ps_c[:, 1, :]]

        def f(ap):
            return ap.bitcast(F32)

        x_loaded = [sem(f"x_loaded{b}") for b in range(B)]
        small_loaded = sem("small_loaded")
        rq_loaded = sem("rq_loaded")
        affine_loaded = sem("affine_loaded")
        adab_loaded = sem("adab_loaded")
        wk_loaded = sem("wk_loaded")
        wo_loaded = sem("wo_loaded")
        adaw_loaded = [sem(f"adaw_loaded{n}") for n in range(6)]
        consts = sem("consts")
        const_step = sem("const_step")
        dve_step = sem("dve_step")
        pro_cols = sem("pro_cols")
        pro_condT = sem("pro_condT")
        pro_blocks = sem("pro_blocks")
        pro_blocks_sb = sem("pro_blocks_sb")
        pro_blocksT = sem("pro_blocksT")
        pro_blocksT_sb = sem("pro_blocksT_sb")
        wT_psum = sem("wT_psum")
        wT_sb = sem("wT_sb")
        pro_keys = sem("pro_keys")
        keys_sb = sem("keys_sb")
        keys_sq = sem("keys_sq")
        keys_mean = sem("keys_mean")
        keys_rms = sem("keys_rms")
        score_col = sem("score_col")
        score_row = sem("score_row")
        score_exp_in = sem("score_exp_in")
        score_exp = sem("score_exp")
        attn_row = sem("attn_row")
        attn_col = sem("attn_col")
        attn_mask = sem("attn_mask")
        att_psum = sem("att_psum")
        att_sb = sem("att_sb")
        proj_psum = sem("proj_psum")
        proj_sb = sem("proj_sb")
        proj_stored = sem("proj_stored")
        proj_loaded = sem("proj_loaded")
        ada_psum = sem("ada_psum")
        ada_sb = sem("ada_sb")
        adaT_psum = sem("adaT_psum")
        ada_cols_sb = sem("ada_cols_sb")
        ada_stored = sem("ada_stored")
        sum_done = sem("sum_done")
        xb_done = sem("xb_done")
        var_ready = sem("var_ready")
        var_eps = sem("var_eps")
        rstd_ready = sem("rstd_ready")
        x_new = sem("x_new")
        x_stored = sem("x_stored")
        hat_done = sem("hat_done")
        x_mod = sem("x_mod")
        xT_stored = [sem(f"xT_stored{n}") for n in range(2)]
        xT_loaded = [sem(f"xT_loaded{n}") for n in range(2)]
        acc_init = [sem(f"acc_init{b}") for b in range(B)]
        raw_loaded = sem("raw_loaded")
        raw_free = sem("raw_free")
        w_scaled = sem("w_scaled")
        w_hi = sem("w_hi")
        w_split = sem("w_split")
        m_done = sem("m_done")
        m_free = sem("m_free")
        hi_done = sem("hi_done")
        s_done = sem("s_done")
        max_done = sem("max_done")
        exp_done = sem("exp_done")
        inv_done = sem("inv_done")
        norm_done = sem("norm_done")
        c_done = sem("c_done")
        c_hi = sem("c_hi")
        c_lo = sem("c_lo")
        pool_waited = sem("pool_waited")
        sp_waited = sem("sp_waited")
        group_cols_set = sem("group_cols_set")
        wide_loaded = [sem(f"wide_loaded{n}") for n in range(2)]
        x_back = sem("x_back")
        res_done = sem("res_done")
        xx_done = sem("xx_done")
        xx_stored = sem("xx_stored")
        h_done = sem("h_done")
        gelu_done = sem("gelu_done")
        h_hi = sem("h_hi")
        h_lo = sem("h_lo")
        xx_loaded = [sem(f"xx_loaded{n}") for n in range(2)]
        fin_done = sem("fin_done")
        out_stored = sem("out_stored")

        def rows(ap, b):
            return ap[b].rearrange("(i p) d -> p i d", p=P)

        ada_v = ada_w.rearrange("(k p) (c n) -> c p k n", p=P, n=512)
        qkv_v = qkv_w.rearrange("(k p) (m g c) -> m g p k c", p=P, m=3, g=G)
        ow_v = out_w.rearrange("(g h p) n -> g p h n", g=G, p=P)
        w1_v = ffn_w1.rearrange("(k p) (g c) -> g p k c", p=P, g=JG)
        w2_v = ffn_w2.rearrange("(g h p) n -> g p h n", g=JG, p=P)

        def bcast(row, parts):
            return row.rearrange("(a n) -> a n", a=1).partition_broadcast(parts)

        def pick(view, g):
            if isinstance(g, int):
                return view[g]
            return view[bass.ds(g, 1)].rearrange("a p k c -> (a p) k c")

        def xT_tile(n):
            return f(xT[:, n].rearrange("p s k t -> p (s k t)"))

        def tiles(b):
            return slice(TT * b, TT * b + TT)

        FFN_AT = [(MV, MQ), (MK, MO), (MV, MQ), (MK, MO)]
        R_MLP = 4 * G
        first_raw = [raw, raw2, raw, raw2]
        ada_buf = [ada_raw[:, n] for n in (0, 1, 2, 3, 2, 3)]

        def hat_tile(stage, b, i):
            if stage:
                return acc[:, TT * b + i, :]
            return (prob if b == 0 else raw)[:, i, :]

        block = ctx.enter_context(nc.Block())

        @block.sync
        def _(sp):
            def store_xT(n, b, m):
                sp.wait_ge(m_free, m)
                sp.dma_start(xT_mid[n][b], xT_tile(b % 2)).then_inc(xT_stored[b % 2], 16)

            def load_xT(src, b):
                sp.dma_start(xT_tile(b % 2), src[b]).then_inc(xT_loaded[b % 2], 16)

            def load_raw(src, g, r):
                sp.wait_ge(raw_free, r)
                sp.sem_inc(sp_waited, 1)
                sp.dma_start(raw[:, :, :], pick(src, g)).then_inc(raw_loaded, 16)

            def init_acc(b, row):
                for i in range(TT):
                    sp.dma_start(acc[:, TT * b + i, :], bcast(row, P)).then_inc(acc_init[b], 16)

            sp.dma_start(cond_sb, cond).then_inc(small_loaded, 16)
            sp.dma_start(bias_rows[0:48, :], qkv_b.rearrange("(r c) -> r c", c=P)).then_inc(small_loaded, 16)
            sp.dma_start(bias_rows[48:64, :], ffn_b1.rearrange("(r c) -> r c", c=P)).then_inc(small_loaded, 16)
            for b in range(B):
                sp.dma_start(acc[:, tiles(b), :], rows(x, b)).then_inc(x_loaded[b], 16)
            sp.dma_start(Wk_sb[:, :, :], Wk.rearrange("(r p) h -> p r h", p=P)).then_inc(wk_loaded, 16)
            sp.dma_start(prob[0:32, 0, :], bcast(rms_w, 32)).then_inc(rq_loaded, 16)
            sp.dma_start(prob[0:32, 1, :], bcast(cond[1], 32)).then_inc(rq_loaded, 16)
            sp.dma_start(Wo_sb[:, :, :], Wo.rearrange("(r p) h -> p r h", p=P)).then_inc(wo_loaded, 16)
            sp.dma_start(raw[:, :, :], pick(qkv_v[MV], 0)).then_inc(raw_loaded, 16)
            sp.dma_start(wide[:, 0, :], bcast(gamma, P)).then_inc(affine_loaded, 16)
            sp.dma_start(wide[:, 1, :], bcast(beta, P)).then_inc(affine_loaded, 16)
            sp.dma_start(ada[:, :], bcast(ada_b, B)).then_inc(adab_loaded, 16)
            for c in range(2):
                sp.dma_start(ada_buf[c], ada_v[c]).then_inc(adaw_loaded[c], 16)
            sp.wait_ge(raw_loaded, 16)
            sp.dma_start(raw2[:, :, :], pick(qkv_v[MK], 0)).then_inc(raw_loaded, 16)
            for c in range(2, 4):
                sp.dma_start(ada_buf[c], ada_v[c]).then_inc(adaw_loaded[c], 16)
            for r, src in ((2, qkv_v[MQ]), (3, ow_v)):
                sp.wait_ge(raw_free, r - 1)
                sp.wait_ge(raw_loaded, 16 * r)
                sp.dma_start(first_raw[r][:, :, :], pick(src, 0)).then_inc(raw_loaded, 16)
            def load_proj(b):
                sp.dma_start(proj[:, :], bcast(proj_mid[b], P)).then_inc(proj_loaded, 16)

            for b in range(1, B):
                sp.wait_ge(proj_sb, b)
                sp.dma_start(proj_mid[b:b + 1, :], proj[32 * b:32 * b + 1, :]).then_inc(proj_stored, 16)
            sp.wait_ge(proj_stored, 16 * (B - 1))
            load_proj(1)
            for c in range(4, 6):
                sp.wait_ge(ada_psum, c - 1)
                sp.dma_start(ada_buf[c], ada_v[c]).then_inc(adaw_loaded[c], 16)
            sp.wait_ge(ada_sb, 6)
            sp.dma_start(ada_mid, ada[:, :]).then_inc(ada_stored, 16)
            for b in range(B):
                sp.wait_ge(x_new, b + 1)
                if b in (1, 2):
                    load_proj(b + 1)
                sp.dma_start(rows(x_mid, b), acc[:, tiles(b), :]).then_inc(x_stored, 16)
                store_xT(0, b, FIRST.at[("X", b, KT - 1)] + 1)
                sp.wait_ge(x_stored, 16 * (b + 1))
                sp.wait_ge(hat_done, TT * (b + 1))
                init_acc(b, out_b)
            for n in range(2):
                sp.wait_ge(xT_stored[n], 32)

            def group(g):
                plan, base = plan_of(g), m_base(g)
                last = plan is LAST

                def used(b):
                    sp.wait_ge(m_done, base + plan.at[("Q", HG * b + 3)] + 1)
                    sp.sem_inc(sp_waited, 1)

                if plan is not FIRST:
                    load_raw(ow_v, g, 4 * g + 3)
                    used(0)
                    load_xT(xT_mid[0], 2)
                if last:
                    sp.wait_ge(ada_stored, 16)
                    for b in range(2):
                        sp.dma_start(wide[:, b, :], bcast(ada_mid[b, 2 * D:3 * D], P)).then_inc(wide_loaded[b], 16)
                    sp.wait_ge(raw_free, 4 * g + 4)
                    sp.dma_start(raw[:, :, :], rows(x_mid, 0)).then_inc(x_back, 16)
                    used(1)
                    load_xT(xT_mid[0], 3)
                    store_xx(0)
                    sp.dma_start(raw[:, :, :], rows(x_mid, 1)).then_inc(x_back, 16)
                    load_gate(2, 2)
                    store_xx(1)
                    load_raw(w1_v, 0, R_MLP)
                    load_gate(3, 2)
                    load_raw(w2_v, 0, R_MLP + 1)
                    return
                if plan is not FIRST:
                    load_raw(qkv_v[MV], g + 1, 4 * g + 4)
                    used(1)
                    load_xT(xT_mid[0], 3)
                    used(2)
                    load_xT(xT_mid[0], 0)
                else:
                    load_xT(xT_mid[0], 0)
                    load_raw(qkv_v[MV], g + 1, 4 * g + 4)
                load_raw(qkv_v[MK], g + 1, 4 * g + 5)
                used(3)
                load_xT(xT_mid[0], 1)
                load_raw(qkv_v[MQ], g + 1, 4 * g + 6)

            def store_xx(b):
                sp.wait_ge(xx_done, TT * (b + 1))
                sp.dma_start(rows(xx_mid, b), raw[:, :, :]).then_inc(xx_stored, 16)
                sp.wait_ge(xx_stored, 16 * (b + 1))

            def load_gate(b, part):
                if part == 2:
                    sp.wait_ge(res_done, TT * (b - 1))
                elif b < 2:
                    sp.wait_ge(res_done, TT * B)
                else:
                    sp.wait_ge(fin_done, TT * (b - 1))
                sp.dma_start(wide[:, b % 2, :], bcast(ada_mid[b, part * D:(part + 1) * D], P)) \
                    .then_inc(wide_loaded[b % 2], 16)

            group(0)
            with sp.Fori(1, G - 1) as g:
                group(g)
            group(G - 1)
            for b in range(2):
                store_xT(1, b, m_base(G - 1) + LAST.at[("X", b, KT - 1)] + 1)
                init_acc(b, ffn_b2)
                if b == 0:
                    sp.wait_ge(raw_free, R_MLP + 2)
                    sp.dma_start(raw[:, :, :], rows(x_mid, 2)).then_inc(x_back, 16)
            store_xx(2)
            sp.dma_start(raw[:, :, :], rows(x_mid, 3)).then_inc(x_back, 16)
            store_xT(1, 2, M_MLP + MLP_PLAN.at[("X", 2, KT - 1)] + 1)
            init_acc(2, ffn_b2)
            store_xx(3)
            load_raw(w1_v, 1, R_MLP + 2)
            load_raw(w2_v, 1, R_MLP + 3)
            store_xT(1, 3, M_MLP + MLP_PLAN.at[("X", 3, KT - 1)] + 1)
            init_acc(3, ffn_b2)
            for n in range(2):
                sp.wait_ge(xT_stored[n], 64)
            for b in range(2):
                load_gate(b, 5)
            sp.wait_ge(xx_stored, 16 * B)
            for u in range(B, B * JG):
                sp.wait_ge(h_done, 4 * (u - 1))
                load_xT(xT_mid[1], u % B)
                jg = u // B + 1
                if jg < JG and u % B == 0:
                    load_raw(w1_v, jg, R_MLP + 2 * jg)
                if jg < JG and u % B == 2:
                    load_raw(w2_v, jg, R_MLP + 2 * jg + 1)
                if u in (B, B + 1):
                    sp.dma_start(xx_in[:, u % B, :, :], rows(xx_mid, u % B)).then_inc(xx_loaded[u % B], 16)
            for b in range(B):
                for i in range(TT):
                    sp.wait_ge(fin_done, TT * b + i + 1)
                    sp.dma_start(out[b, P * i:P * i + P, :], acc[:, TT * b + i, :]).then_inc(out_stored, 16)
                if b < 2:
                    load_gate(b + 2, 5)
                    sp.dma_start(xx_in[:, b, :, :], rows(xx_mid, b + 2)).then_inc(xx_loaded[b], 16)
            sp.wait_ge(out_stored, 16 * B * TT)

        def piece(mat, q):
            return (lambda t: t[:, :, P * q:P * q + P]) if mat in (MQ, MK) else (lambda t: t[:, q, :])

        @block.gpsimd
        def _(pool):
            step = [0]

            def link(ins):
                step[0] += 1
                ins.then_inc(const_step, 1)
                pool.wait_ge(const_step, step[0])

            def hold(semaphore, value):
                pool.wait_ge(semaphore, value)
                pool.sem_inc(pool_waited, 1)

            link(nc.gpsimd.memset(ident[:, :], 0.0))
            link(nc.gpsimd.affine_select(out=ident[:, :], in_=ident[:, :], compare_op=ALU.not_equal, fill=1.0,
                                         base=0, pattern=[[-1, P]], channel_multiplier=1))
            link(nc.gpsimd.memset(block_ind[:, :], 0.0))
            link(nc.gpsimd.memset(block_ind[0:BLK, 30:31], 1.0))
            link(nc.gpsimd.memset(block_ind[BLK:P, 31:32], 1.0))
            link(nc.gpsimd.memset(batch_mask[:, :], 1.0))
            link(nc.gpsimd.affine_select(out=batch_mask[:, :], in_=batch_mask[:, :], compare_op=ALU.is_ge, fill=0.0,
                                         base=0, pattern=[[-NBLK, B]], channel_multiplier=1))
            link(nc.gpsimd.affine_select(out=batch_mask[:, :], in_=batch_mask[:, :], compare_op=ALU.is_ge, fill=0.0,
                                         base=NBLK - 1, pattern=[[NBLK, B]], channel_multiplier=-1))
            link(nc.gpsimd.memset(minus_half[:, :], -0.5))
            nc.gpsimd.memset(one[:, :], 1.0).then_inc(consts, 1)

            def split(mat, dst, q, r, scale, src_of):
                at = piece(mat, q)
                src, hi, lo = at(src_of), at(W[:, dst, HI]), at(W[:, dst, LO])
                if scale != 1.0:
                    nc.gpsimd.tensor_scalar(src, src, scale, 1.0, ALU.mult, ALU.mult).then_inc(w_scaled, 1)
                    hold(w_scaled, r - 2 + q + 1)
                nc.gpsimd.tensor_scalar(hi, src, 1.0, 1.0, ALU.mult, ALU.mult).then_inc(w_hi, 1)
                hold(w_hi, 4 * r + q + 1)
                nc.gpsimd.tensor_tensor(lo, src, f(hi), ALU.subtract).then_inc(w_split, 1)

            def split_pieces(mat, dst, r, pieces=range(4), scale=1.0, wait=None, src=raw):
                for q in pieces:
                    if q == 0:
                        hold(raw_loaded, 16 * (r + 1))
                    if wait is not None:
                        wait(q)
                    split(mat, dst, q, r, scale, src)
                    if q == 3:
                        hold(w_split, 4 * (r + 1))
                        pool.sem_inc(raw_free, 1)

            def inverse_std(call):
                pool.wait_ge(var_ready, call + 1)
                nc.gpsimd.tensor_scalar(rstd[:, :], mean_var[:, :, 1], 1.0, EPS, ALU.mult, ALU.add).then_inc(var_eps, 1)
                pool.wait_ge(var_eps, call + 1)
                nc.gpsimd.tensor_tensor(rstd[:, :], rstd[:, :], minus_half[:, :], ALU.pow).then_inc(rstd_ready, 1)

            def add_beta(b):
                for i in range(TT):
                    pool.wait_ge(sum_done, TT * b + i + 1)
                    nc.gpsimd.tensor_tensor(acc[:, TT * b + i, :], acc[:, TT * b + i, :], wide[:, 1, :],
                                            ALU.add).then_inc(xb_done, 1)

            def add_xx(b):
                pool.wait_ge(x_back, 16 * (b + 1))
                for i in range(TT):
                    pool.wait_ge(res_done, TT * b + i + 1)
                    nc.gpsimd.tensor_tensor(raw[:, i, :], raw[:, i, :], acc[:, TT * b + i, :],
                                            ALU.add).then_inc(xx_done, 1)

            split_pieces(MV, MV, 0)
            pool.wait_ge(keys_mean, 1)
            nc.gpsimd.tensor_tensor(small[:, 3:4], small[:, 1:2], minus_half[0:32, 0:1], ALU.pow).then_inc(keys_rms, 1)
            split_pieces(MK, MK, 1, src=raw2)
            split_pieces(MQ, MQ, 2, scale=SCALE)
            pool.wait_ge(affine_loaded, 32)
            add_beta(0)
            inverse_std(0)
            inverse_std(1)
            split_pieces(MO, MO, 3, src=raw2)

            def normalise(g, n):
                for t in range(TT):
                    hold(inv_done, NS * g + TT * n + t + 1)
                    nc.gpsimd.tensor_scalar(prob[:, t, :], prob[:, t, :], row_inv[:, t:t + 1], 1.0,
                                            ALU.mult, ALU.mult).then_inc(norm_done, 1)

            def group(g):
                plan, base = plan_of(g), m_base(g)
                last = plan is LAST

                def used(tile):
                    return lambda q: hold(m_done, base + plan.at[tile] + 1)

                def head_used(q):
                    hold(m_done, base + plan.at[("Q", 12 + q)] + 1)

                for n in range(SLOTS):
                    if n == 13:
                        if last:
                            split_pieces(MQ, MV, 4 * g + 4, wait=used(("V", 3, 3)))
                        else:
                            split_pieces(MV, MV, 4 * g + 4, wait=used(("V", 3, 3)))
                    if n == 14 and not last:
                        split_pieces(MK, MK, 4 * g + 5, range(0, 2), wait=head_used)
                    if n == 15 and not last:
                        split_pieces(MK, MK, 4 * g + 5, range(2, 3), wait=head_used)
                    normalise(g, n)
                    if plan is FIRST:
                        if n == 0:
                            add_beta(1)
                            inverse_std(2)
                        if n == 1:
                            inverse_std(3)
                        if n in (4, 8):
                            add_beta(n // HG + 1)
                            inverse_std(2 * (n // HG) + 2)
                            inverse_std(2 * (n // HG) + 3)
                    elif n == 2:
                        split_pieces(MO, MO, 4 * g + 3, wait=lambda q: hold(m_done, base + 1))
                    if last and n in (7, 11):
                        add_xx(n // HG - 1)
                        inverse_std(2 * B + n // HG - 1)
                if last:
                    split_pieces(MO, MQ, 4 * g + 5, wait=lambda q: head_used(3))
                else:
                    split_pieces(MK, MK, 4 * g + 5, range(3, 4), wait=head_used)
                    split_pieces(MQ, MQ, 4 * g + 6, scale=SCALE, wait=head_used)

            group(0)
            with pool.Fori(1, G - 1) as g:
                group(g)
            group(G - 1)
            for b in (2, 3):
                add_xx(b)
                inverse_std(2 * B + b)
            for jg in range(1, JG):
                split_pieces(MQ, FFN_AT[jg][0], R_MLP + 2 * jg,
                             wait=lambda q: pool.wait_ge(h_done, 4 * B * (jg - 1)) if jg > 1 else None)
                split_pieces(MO, FFN_AT[jg][1], R_MLP + 2 * jg + 1,
                             wait=lambda q: pool.wait_ge(m_done, M_MLP + MLP_PLAN.at[("Z", B * jg - B - 1, TT - 1)] + 1
                                                         if jg > 1 else M_MLP))

        def act_take(act, plan, m0, tile):
            act.wait_ge(m_done, m0 + plan.at[tile] + 1)

        @block.scalar
        def _(act):
            for m in range(2):
                for k in range(KT):
                    act.wait_ge(wT_psum, KT * m + k + 1)
                    nc.scalar.copy((WkT, WoT)[m][:, k, :], four[k]).then_inc(wT_sb, 1)
            act.wait_ge(keys_sb, 1)
            nc.scalar.activation(prob[0:32, 3, :], prob[0:32, 2, :], ACT.Square,
                                 accum_out=small[:, 0:1]).then_inc(keys_sq, 1)
            act.wait_ge(score_exp_in, 1)
            nc.scalar.activation(small_row[:, 32:64], small_row[:, 32:64], ACT.Exp).then_inc(score_exp, 1)
            for b in range(1, B):
                act.wait_ge(proj_psum, b + 1)
                row = slice(32 * b, 32 * b + 1)
                nc.scalar.copy(proj[row, :], ps_m[row, b, :]).then_inc(proj_sb, 1)

            def hi(dst, bank, bias):
                if bias is None:
                    nc.scalar.copy(dst, bank).then_inc(hi_done, 1)
                else:
                    nc.scalar.activation(dst, bank, ACT.Identity, bias=bias).then_inc(hi_done, 1)

            mods = [0]

            def modulate(stage, b, k, bank):
                if b >= 2 or stage:
                    act.wait_ge(xT_stored[b % 2], 16 * (b // 2 + 2 * stage))
                mods[0] += 1
                nc.scalar.activation(bank, bank, ACT.Identity, bias=ada_cols[:, 2 * stage, k, b:b + 1],
                                     scale=ada_cols[:, 2 * stage + 1, k, b:b + 1]).then_inc(x_mod, 1)
                act.wait_ge(x_mod, mods[0])
                hi(xT[:, b % 2, HI, k, :], bank, None)

            def group(g):
                plan, base = plan_of(g), m_base(g)
                if plan is not FIRST:
                    act.wait_ge(group_cols_set, g + 1)
                for tile in plan.done:
                    kind, n = tile[0], tile[1]
                    if tile in plan.hi_at:
                        act.wait_ge(m_done, base + plan.at[tile] + 1)
                    bank = ps_m[:, plan.at[tile] % 4, :] if tile in plan.at else None
                    h = n % HG
                    if tile == ("K", 0) and plan is FIRST:
                        act.wait_ge(group_cols_set, 1)
                        act.wait_ge(ada_stored, 16)
                    if kind == "X":
                        if plan is FIRST and n == 0 and tile[2] == 0:
                            act.wait_ge(ada_cols_sb, 2)
                        modulate(0 if plan is FIRST else 1, n, tile[2], bank)
                    elif kind == "K":
                        hi(QK[:, 1, HI, :], bank, group_cols[:, HG + h:HG + h + 1])
                    elif kind == "Q":
                        hi(QK[:, 0, HI, :], bank, group_cols[:, h:h + 1])
                    elif kind == "V":
                        hi(V[:, HI, tile[2], :], bank, None)
                    elif kind == "O":
                        hi(O[:, HI, h, :], bank, group_cols[:, 2 * HG + h:2 * HG + h + 1])
                    elif kind == "S":
                        t = tile[2]
                        act.wait_ge(max_done, NS * g + TT * n + t + 1)
                        nc.scalar.activation(prob[:, t, :], ps_s[:, (TT * n + t) % 2, :], ACT.Exp,
                                             bias=neg_max[:, t:t + 1],
                                             accum_out=row_sum[:, t:t + 1]).then_inc(exp_done, 1)
                    elif kind == "C":
                        j = tile[2]
                        act.wait_ge(c_done, NS * g + TT * n + j + 1)
                        nc.scalar.copy(probT[:, HI, j, :], ps_c[:, (TT * n + j) % 2, :]).then_inc(c_hi, 1)

            group(0)
            with act.Fori(1, G - 1) as g:
                group(g)
            group(G - 1)
            for tile in MLP_PLAN.done:
                kind, u = tile[0], tile[1]
                if kind == "X":
                    act.wait_ge(m_done, M_MLP + MLP_PLAN.at[tile] + 1)
                    modulate(1, u, tile[2], ps_m[:, MLP_PLAN.at[tile] % 4, :])
                elif kind == "H":
                    j = tile[2]
                    n = 4 * u + j
                    act.wait_ge(h_done, n + 1)
                    if n >= 4:
                        act.wait_ge(h_lo, n - 3)
                    nc.scalar.activation(prob[:, j, :], four[j], ACT.Gelu,
                                         bias=cols[:, 3 * H + 4 * (u // B) + j:3 * H + 4 * (u // B) + j + 1]) \
                        .then_inc(gelu_done, 1)

        @block.vector
        def _(dve):
            count = [0]

            def link(ins):
                count[0] += 1
                ins.then_inc(dve_step, 1)
                dve.wait_ge(dve_step, count[0])

            v = nc.vector
            dve.wait_ge(pro_cols, 1)
            link(v.tensor_copy(cols[:, :], ps_m[:, 0, 0:64]))
            link(v.tensor_scalar(cols[:, 0:H], cols[:, 0:H], SCALE, None, ALU.mult))
            v.tensor_copy(condT[:, :, :], ps_m[:, 1, 0:16].rearrange("p (k b) -> p k b", b=B)).then_inc(pro_condT, 1)
            dve.wait_ge(pro_blocks, 1)
            v.tensor_copy(blocks[:, :], ps_m[0:32, 2, :]).then_inc(pro_blocks_sb, 1)
            dve.wait_ge(pro_blocksT, 1)
            v.tensor_copy(blocksT[:, :, :], ps_m[:, 3, 0:128].rearrange("p (k n) -> p k n", n=32)) \
                .then_inc(pro_blocksT_sb, 1)
            dve.wait_ge(rq_loaded, 32)
            link(v.tensor_tensor(prob[0:32, 1, :], prob[0:32, 1, :], prob[0:32, 0, :], ALU.mult))
            dve.wait_ge(pro_keys, 1)
            v.tensor_copy(prob[0:32, 2, :], ps_m[0:32, 0, :]).then_inc(keys_sb, 1)
            dve.wait_ge(keys_sb, 1)
            link(v.tensor_tensor(prob[0:32, 0, :], prob[0:32, 1, :], prob[0:32, 2, :], ALU.mult))
            link(v.reduce_sum(small[:, 2:3], prob[0:32, 0, :], axis=AX_X))
            dve.wait_ge(keys_sq, 1)
            v.tensor_scalar(small[:, 1:2], small[:, 0:1], 1.0 / D, EPS, ALU.mult, ALU.add).then_inc(keys_mean, 1)
            dve.wait_ge(keys_rms, 1)
            v.tensor_tensor(small[:, 4:5], small[:, 2:3], small[:, 3:4], ALU.mult).then_inc(score_col, 1)
            dve.wait_ge(score_row, 1)
            r = small_row
            scores = ps_m[0:1, 1, 64:96].rearrange("p (b n) -> p b n", n=NBLK)
            expd = r[:, 32:64].rearrange("p (b n) -> p b n", n=NBLK)
            link(v.tensor_reduce(r[:, 0:4], scores, axis=AX_X, op=ALU.max))
            v.tensor_tensor(expd, scores, r[:, 0:4].unsqueeze(2).to_broadcast([1, B, NBLK]),
                            ALU.subtract).then_inc(score_exp_in, 1)
            dve.wait_ge(score_exp, 1)
            link(v.reduce_sum(r[:, 4:8], expd, axis=AX_X))
            link(v.reciprocal(r[:, 8:12], r[:, 4:8]))
            v.tensor_tensor(r[:, 64:96].rearrange("p (b n) -> p b n", n=NBLK), expd,
                            r[:, 8:12].unsqueeze(2).to_broadcast([1, B, NBLK]), ALU.mult).then_inc(attn_row, 1)
            dve.wait_ge(attn_col, 1)
            link(v.tensor_copy(small[:, 5:6], ps_m[0:32, 1, 100:101]))
            v.tensor_scalar(small[:, 8:12], batch_mask[:, :], small[:, 5:6], None, ALU.mult).then_inc(attn_mask, 1)
            dve.wait_ge(att_psum, 1)
            dve.wait_ge(wT_psum, KT)
            att = ps_m[:, 1, 128:144]
            for k in range(KT):
                last = v.tensor_copy(att_bc[:, k], att[:, B * k:B * k + B].unsqueeze(2).to_broadcast([P, B, P]))
                if k < KT - 1:
                    link(last)
            last.then_inc(att_sb, 1)

            def add_ada(c):
                dve.wait_ge(ada_psum, c + 1)
                v.tensor_tensor(ada[:, 512 * c:512 * c + 512], ada[:, 512 * c:512 * c + 512],
                                four[c % 4][0:B, :], ALU.add).then_inc(ada_sb, 1)

            def ada_columns(half):
                dve.wait_ge(adaT_psum, half + 1)
                link(v.tensor_copy(ada_cols[:, 2 * half:2 * half + 2],
                                   four[2][:, 32 * half:32 * half + 32].rearrange("p (y k b) -> p y k b", y=2, k=KT)))
                v.tensor_scalar(ada_cols[:, 2 * half + 1], ada_cols[:, 2 * half + 1], 1.0, None,
                                ALU.add).then_inc(ada_cols_sb, 2 - half)

            dve.wait_ge(adab_loaded, 16)
            add_ada(0)
            add_ada(1)
            ada_columns(0)

            def moments(src, i):
                link(v.bn_stats(stats[:, i, :], src))
                last = v.bn_aggr(mean_var[:, i, :], stats[:, i, :])
                if i < TT - 1:
                    link(last)
                else:
                    last.then_inc(var_ready, 1)

            def norm_step(stage, tile):
                kind, b, i = tile
                z, a = hat_tile(stage, b, i), acc[:, TT * b + i, :]
                mean, inv = mean_var[:, i, 0:1], rstd[:, i:i + 1]
                if kind == "sum":
                    if b == 0:
                        dve.wait_ge(proj_psum, 1)
                        src = ps_m[:, 0, :]
                    else:
                        if i == 0:
                            dve.wait_ge(proj_loaded, 16 * b)
                            if b == 1:
                                dve.wait_ge(raw_free, 4)
                            else:
                                dve.wait_ge(m_done, FIRST.at[("X", b - 1, KT - 1)] + 1)
                        src = proj[:, :]
                    v.tensor_tensor(z, a, src, ALU.add).then_inc(sum_done, 1)
                    dve.wait_ge(sum_done, TT * b + i + 1)
                    moments(z, i)
                elif kind == "aff":
                    if i == 0:
                        dve.wait_ge(rstd_ready, 2 * b + 1)
                        dve.wait_ge(affine_loaded, 32)
                    link(v.scalar_tensor_tensor(out=z, in0=z, scalar=mean, in1=wide[:, 0, :],
                                                op0=ALU.subtract, op1=ALU.mult))
                    dve.wait_ge(xb_done, TT * b + i + 1)
                    link(v.scalar_tensor_tensor(out=a, in0=z, scalar=inv, in1=a, op0=ALU.mult, op1=ALU.add))
                    if i == TT - 1:
                        dve.sem_inc(x_new, 1)
                    moments(a, i)
                elif kind == "res":
                    if i == 0:
                        dve.wait_ge(wide_loaded[b % 2], 16 * (b // 2 + 1))
                        dve.wait_ge(x_back, 16 * (b + 1))
                    link(v.tensor_tensor(a, a, wide[:, b % 2, :], ALU.mult))
                    v.tensor_tensor(a, a, raw[:, i, :], ALU.add).then_inc(res_done, 1)
                    dve.wait_ge(res_done, TT * b + i + 1)
                    moments(a, i)
                else:
                    if i == 0:
                        dve.wait_ge(rstd_ready, 2 * B + b + 1 if stage else 2 * b + 2)
                    if stage:
                        dve.wait_ge(xx_done, TT * b + i + 1)
                    v.tensor_scalar(z, a, mean, inv, ALU.subtract, ALU.mult).then_inc(hat_done, 1)

            for kind in ("sum", "aff", "hat"):
                for i in range(TT):
                    norm_step(0, (kind, 0, i))
            for c in range(2, 6):
                add_ada(c)

            def inverse(g, s):
                dve.wait_ge(exp_done, NS * g + s + 1)
                v.reciprocal(row_inv[:, s % TT:s % TT + 1], row_sum[:, s % TT:s % TT + 1]).then_inc(inv_done, 1)

            def lo(dst, hi_part, bank, bias):
                if bias is None:
                    v.tensor_tensor(dst, bank, f(hi_part), ALU.subtract).then_inc(m_free, 1)
                else:
                    v.scalar_tensor_tensor(out=dst, in0=bank, scalar=bias, in1=f(hi_part), op0=ALU.add,
                                           op1=ALU.subtract).then_inc(m_free, 1)

            def set_group_cols(g):
                at = slice(0, HG) if isinstance(g, int) and g == 0 else bass.ds(HG * g, HG)
                v.tensor_copy(group_cols[:, :].rearrange("p (m h) -> p m h", m=3),
                              cols[:, 0:3 * H].rearrange("p (m h) -> p m h", m=3)[:, :, at]) \
                    .then_inc(group_cols_set, 1)
                dve.wait_ge(group_cols_set, g + 1)

            def group(g):
                plan, base, his = plan_of(g), m_base(g), hi_base(g)
                extra = {FIRST: FIRST_EXTRA, LAST: LAST_EXTRA}.get(plan, {})
                set_group_cols(g)
                for tile in after(plan.done, extra):
                    kind, n = tile[0], tile[1]
                    bank = ps_m[:, plan.at[tile] % 4, :] if tile in plan.at else None
                    h = n % HG
                    if tile in plan.hi_at:
                        dve.wait_ge(hi_done, his + plan.hi_at[tile] + 1)
                    if kind == "X":
                        lo(xT[:, n % 2, LO, tile[2], :], xT[:, n % 2, HI, tile[2], :], bank, None)
                        if plan is FIRST and n == 0 and tile[2] == KT - 1:
                            ada_columns(1)
                    elif kind == "K":
                        lo(QK[:, 1, LO, :], QK[:, 1, HI, :], bank, group_cols[:, HG + h:HG + h + 1])
                    elif kind == "Q":
                        lo(QK[:, 0, LO, :], QK[:, 0, HI, :], bank, group_cols[:, h:h + 1])
                    elif kind == "V":
                        lo(V[:, LO, tile[2], :], V[:, HI, tile[2], :], bank, None)
                    elif kind == "O":
                        lo(O[:, LO, h, :], O[:, HI, h, :], bank, group_cols[:, 2 * HG + h:2 * HG + h + 1])
                    elif kind == "Y":
                        at = TT * n + tile[2]
                        dve.wait_ge(m_done, base + plan.at[tile] + 1)
                        if plan is FIRST and tile[2] == 0:
                            dve.wait_ge(acc_init[n], 16 * TT)
                        v.tensor_tensor(acc[:, at, :], acc[:, at, :], bank, ALU.add).then_inc(m_free, 1)
                    elif kind == "S":
                        s = TT * n + tile[2]
                        dve.wait_ge(s_done, NS * g + s + 1)
                        v.tensor_reduce(neg_max[:, s % TT:s % TT + 1], ps_s[:, s % 2, :], axis=AX_X, op=ALU.max,
                                        negate=True).then_inc(max_done, 1)
                        if tile[2] >= 1:
                            inverse(g, s - 1)
                        if tile[2] == TT - 1:
                            inverse(g, s)
                    elif kind == "C":
                        j = tile[2]
                        dve.wait_ge(c_hi, NS * g + TT * n + j + 1)
                        v.tensor_tensor(probT[:, LO, j, :], ps_c[:, (TT * n + j) % 2, :], f(probT[:, HI, j, :]),
                                        ALU.subtract).then_inc(c_lo, 1)
                    else:
                        norm_step(0 if plan is FIRST else 1, tile)

            group(0)
            with dve.Fori(1, G - 1) as g:
                group(g)
            group(G - 1)
            for tile in after(MLP_PLAN.done, MLP_EXTRA):
                kind, u = tile[0], tile[1]
                bank = ps_m[:, MLP_PLAN.at[tile] % 4, :] if tile in MLP_PLAN.at else None
                if kind == "X":
                    dve.wait_ge(hi_done, HI_MLP + MLP_PLAN.hi_at[tile] + 1)
                    lo(xT[:, u % 2, LO, tile[2], :], xT[:, u % 2, HI, tile[2], :], bank, None)
                elif kind == "H":
                    j = tile[2]
                    n = 4 * u + j
                    dve.wait_ge(gelu_done, n + 1)
                    v.tensor_copy(hid[u % 2][:, HI, j, :], prob[:, j, :]).then_inc(h_hi, 1)
                    dve.wait_ge(h_hi, n + 1)
                    v.tensor_tensor(hid[u % 2][:, LO, j, :], prob[:, j, :], f(hid[u % 2][:, HI, j, :]),
                                    ALU.subtract).then_inc(h_lo, 1)
                elif kind == "Z":
                    b, i = u % B, tile[2]
                    a = acc[:, TT * b + i, :]
                    dve.wait_ge(m_done, M_MLP + MLP_PLAN.at[tile] + 1)
                    if u < B and i == 0:
                        dve.wait_ge(acc_init[b], 2 * 16 * TT)
                    v.tensor_tensor(a, a, bank, ALU.add).then_inc(m_free, 1)
                    if u >= B * JG - B:
                        dve.wait_ge(m_free, M_MLP + MLP_PLAN.at[tile] + 1)
                        if i == 0:
                            dve.wait_ge(wide_loaded[b % 2], 16 * (2 + b // 2 + 1))
                            dve.wait_ge(xx_loaded[b % 2], 16 * (b // 2 + 1))
                        link(v.tensor_tensor(a, a, wide[:, b % 2, :], ALU.mult))
                        v.tensor_tensor(a, a, xx_in[:, b % 2, i, :], ALU.add).then_inc(fin_done, 1)
                else:
                    norm_step(1, tile)

        @block.tensor
        def _(pe):
            mm, tr = nc.tensor.matmul, nc.tensor.transpose
            pe.wait_ge(consts, 1)
            pe.wait_ge(small_loaded, 48)
            tr(ps_m[:, 0, 0:64], bias_rows[:, :], ident[0:64, 0:64])
            for k in range(KT):
                last = tr(ps_m[:, 1, B * k:B * k + B], cond_sb[:, P * k:P * k + P], ident[0:B, 0:B])
            last.then_inc(pro_cols, 1)
            for b in range(B):
                pe.wait_ge(x_loaded[b], 16)
                for i in range(TT):
                    n = TT * b + i
                    last = mm(ps_m[0:32, 2, :], block_ind[:, 30 - 2 * n:62 - 2 * n], acc[:, n, :],
                              start=(n == 0), stop=(n == B * TT - 1))
            last.then_inc(pro_blocks, 1)

            def transpose_weights(m):
                pe.wait_ge((wk_loaded, wo_loaded)[m], 16)
                for k in range(KT):
                    if m:
                        pe.wait_ge(wT_sb, k + 1)
                    for r in range(KT):
                        last = tr(four[k][:, P * r:P * r + P], (Wk_sb, Wo_sb)[m][:, r, P * k:P * k + P], ident[:, :])
                    last.then_inc(wT_psum, 1)

            transpose_weights(0)
            pe.wait_ge(pro_blocks_sb, 1)
            for k in range(KT):
                last = tr(ps_m[:, 3, 32 * k:32 * k + 32], blocks[:, P * k:P * k + P], ident[0:32, 0:32])
            last.then_inc(pro_blocksT, 1)
            pe.wait_ge(pro_blocksT_sb, 1)
            pe.wait_ge(pro_condT, 1)
            pe.wait_ge(wT_sb, KT)
            for k in range(KT):
                last = mm(ps_m[0:32, 0, :], blocksT[:, k, :], WkT[:, k, :], start=(k == 0), stop=(k == KT - 1))
            last.then_inc(pro_keys, 1)
            transpose_weights(1)
            pe.wait_ge(score_col, 1)
            tr(ps_m[0:1, 1, 64:96], small[:, 4:5], ident[0:32, 0:32]).then_inc(score_row, 1)
            pe.wait_ge(attn_row, 1)
            mm(ps_m[0:32, 1, 100:101], small_row[:, 64:96], one[:, :], start=True, stop=True).then_inc(attn_col, 1)
            pe.wait_ge(attn_mask, 1)
            for k in range(KT):
                last = mm(ps_m[:, 1, 128 + B * k:128 + B * k + B], blocks[:, P * k:P * k + P], small[:, 8:12],
                          start=True, stop=True)
            last.then_inc(att_psum, 1)
            pe.wait_ge(att_sb, 1)
            pe.wait_ge(wT_sb, 2 * KT)

            def project(b):
                for k in range(KT):
                    last = mm(ps_m[:, b, :], att_bc[:, k, b, :], WoT[:, k, :], start=(k == 0), stop=(k == KT - 1))
                last.then_inc(proj_psum, 1)

            def ada_chunk(c):
                pe.wait_ge(adaw_loaded[c], 16)
                if c >= 4:
                    pe.wait_ge(ada_sb, c - 3)
                if c == 2:
                    pe.wait_ge(ada_cols_sb, 2)
                for k in range(KT):
                    last = mm(four[c % 4][0:B, :], condT[:, k, :], ada_buf[c][:, k, :],
                              start=(k == 0), stop=(k == KT - 1))
                last.then_inc(ada_psum, 1)

            def ada_transpose(half):
                pe.wait_ge(ada_sb, 2 if half == 0 else 6)
                for y in range(2):
                    for k in range(KT):
                        at, part = 32 * half + 16 * y + B * k, 3 * half + y
                        last = tr(four[2][:, at:at + B], ada[:, 512 * part + P * k:512 * part + P * k + P],
                                  ident[0:B, 0:B])
                last.then_inc(adaT_psum, 1)

            project(0)
            ada_chunk(0)
            ada_chunk(1)
            for b in range(1, B):
                project(b)
            ada_transpose(0)
            for c in range(2, 6):
                ada_chunk(c)

            def product(out_ap, stationary, moving, k0, k1, last_k):
                for k in range(k0, k1):
                    for n, (a, c) in enumerate(PAIRS):
                        last = mm(out_ap, stationary(a, k), moving(c, k), start=(k == 0 and n == 0),
                                  stop=(k == last_k - 1 and n == len(PAIRS) - 1))
                return last

            def transpose_x(stage, b, k, bank):
                if k == 0:
                    pe.wait_ge(hat_done, TT * (B * stage + b + 1))
                for i in range(TT):
                    last = tr(bank[:, P * i:P * i + P], hat_tile(stage, b, i)[:, P * k:P * k + P], ident[:, :])
                last.then_inc(m_done, 1)

            def group(g):
                plan, base = plan_of(g), m_base(g)
                for s in plan.order:
                    kind, n = s[0], s[1]
                    b, h = n // HG, n % HG
                    xb = xT[:, (b if kind in "KQ" else n) % 2]
                    tile = ("O", n) if kind == "D" else (s[0], s[1]) if kind in "KQ" else s
                    if tile in plan.at:
                        m = plan.at[tile]
                        bank = ps_m[:, m % 4, :]
                        first = s[2] == 0 if kind in "KQD" else True
                        if first and m >= 4:
                            pe.wait_ge(m_free, base + m - 3)
                    if kind == "X":
                        if plan is FIRST and n == 0 and s[2] == 0:
                            pe.wait_ge(proj_sb, B - 1)
                        transpose_x(0 if plan is FIRST else 1, n, s[2], bank)
                        if plan is FIRST and n == 0 and s[2] == KT - 1:
                            ada_transpose(1)
                    elif kind in "KQ":
                        if s[2] == 0 and h == 0 and kind == "K":
                            if plan is FIRST:
                                pe.wait_ge(m_free, plan.at[("X", b, KT - 1)] + 1)
                            else:
                                pe.wait_ge(xT_loaded[b % 2], 16 * (2 * (g - 1) + b // 2 + 1))
                        mat = MK if kind == "K" else MQ
                        if s[2] == 0 and b == 0:
                            pe.wait_ge(w_split, 16 * g + (4 if kind == "K" else 8) + h + 1)
                        last = product(bank, lambda a, k: W[:, mat, a, k, P * h:P * h + P],
                                       lambda c, k: xb[:, c, k, :], s[2], s[3], KT)
                        if s[3] == KT:
                            last.then_inc(m_done, 1)
                    elif kind == "V":
                        j = s[2]
                        product(bank, lambda a, k: xb[:, a, k, P * j:P * j + P],
                                lambda c, k: W[:, MV, c, k, :], 0, KT, KT).then_inc(m_done, 1)
                    elif kind == "Y":
                        i = s[2]
                        if i == 0:
                            pe.wait_ge(w_split, 16 * g + 16)
                            pe.wait_ge(m_free, base + plan.at[("O", HG * n + 3)] + 1)
                        product(bank, lambda a, k: O[:, a, k, P * i:P * i + P],
                                lambda c, k: W[:, MO, c, k, :], 0, HG, HG).then_inc(m_done, 1)
                    elif kind == "S":
                        t = s[2]
                        if t == 0:
                            pe.wait_ge(m_free, base + plan.at[("Q", n)] + 1)
                        if plan is FIRST and n == 0 and t == 0:
                            pe.wait_ge(ada_cols_sb, 3)
                        if TT * n + t >= 2:
                            pe.wait_ge(exp_done, NS * g + TT * n + t - 1)
                        product(ps_s[:, (TT * n + t) % 2, :], lambda a, k: QK[:, 0, a, P * t:P * t + P],
                                lambda c, k: QK[:, 1, c, :], 0, 1, 1).then_inc(s_done, 1)
                    elif kind == "C":
                        j = s[2]
                        if j == 0:
                            pe.wait_ge(norm_done, NS * g + TT * n + TT)
                        if TT * n + j >= 2:
                            pe.wait_ge(c_lo, NS * g + TT * n + j - 1)
                        for t in range(TT):
                            last = tr(ps_c[:, (TT * n + j) % 2, P * t:P * t + P], prob[:, t, P * j:P * j + P],
                                      ident[:, :])
                        last.then_inc(c_done, 1)
                    elif kind == "D":
                        j = s[2]
                        if j == 0 and h == 0:
                            pe.wait_ge(m_free, base + plan.at[("V", b, TT - 1)] + 1)
                        pe.wait_ge(c_lo, NS * g + TT * n + j + 1)
                        last = product(bank, lambda a, k: V[:, a, k, P * h:P * h + P],
                                       lambda c, k: probT[:, c, k, :], j, j + 1, TT)
                        if j == TT - 1:
                            last.then_inc(m_done, 1)
                pe.wait_ge(m_free, base + plan.tiles)

            group(0)
            with pe.Fori(1, G - 1) as g:
                group(g)
            group(G - 1)
            for s in MLP_PLAN.order:
                kind, u = s[0], s[1]
                b, jg = u % B, u // B
                if s in MLP_PLAN.at:
                    m = MLP_PLAN.at[s]
                    bank = ps_m[:, m % 4, :]
                    if m >= 4:
                        pe.wait_ge(m_free, M_MLP + m - 3)
                if kind == "X":
                    transpose_x(1, u, s[2], bank)
                elif kind == "H":
                    j = s[2]
                    n = 4 * u + j
                    w1 = FFN_AT[jg][0]
                    if j == 0 and u < 2:
                        pe.wait_ge(m_free, m_base(G - 1) + LAST.at[("X", u, KT - 1)] + 1)
                    elif j == 0 and u < B:
                        pe.wait_ge(m_free, M_MLP + MLP_PLAN.at[("X", u, KT - 1)] + 1)
                    elif j == 0:
                        pe.wait_ge(xT_loaded[b % 2], 16 * (2 * (G - 1) + 2 * (jg - 1) + b // 2 + 1))
                    if b == 0:
                        pe.wait_ge(w_split, 4 * (R_MLP + 2 * jg) + j + 1)
                    if n >= 4:
                        pe.wait_ge(gelu_done, n - 3)
                    product(four[j], lambda a, k: W[:, w1, a, k, P * j:P * j + P],
                            lambda c, k: xT[:, b % 2, c, k, :], 0, KT, KT).then_inc(h_done, 1)
                else:
                    i = s[2]
                    w2 = FFN_AT[jg][1]
                    if i == 0:
                        pe.wait_ge(h_lo, 4 * u + 4)
                        if b == 0:
                            pe.wait_ge(w_split, 4 * (R_MLP + 2 * jg + 2))
                    product(bank, lambda a, k: hid[u % 2][:, a, k, P * i:P * i + P],
                            lambda c, k: W[:, w2, c, k, :], 0, 4, 4).then_inc(m_done, 1)


_INS = ["x", "cond_2048", "L0_cond_rms_weight", "L0_cond_Wk", "L0_cond_Wo", "L0_cond_ln_gamma", "L0_cond_ln_beta",
        "L1_cond_ada_w", "L1_cond_ada_b", "L1_cond_qkv_w", "L1_cond_qkv_b", "L1_cond_out_w", "L1_cond_out_b",
        "L1_cond_ffn_w1", "L1_cond_ffn_b1", "L1_cond_ffn_w2", "L1_cond_ffn_b2"]


def kernel(**inputs):
    import numpy as _np
    import concourse.bacc as _bacc
    from concourse import mybir as _mybir
    from concourse.bass_utils import run_bass_kernel_spmd as _run

    nc = _bacc.Bacc("TRN2", target_bir_lowering=False, num_devices=1)
    arrays, args = {}, []
    for name in _INS:
        a = _np.ascontiguousarray(inputs[name])
        arrays[f"in_{name}"] = a
        args.append(nc.dram_tensor(f"in_{name}", a.shape, _mybir.dt.from_np(a.dtype), kind="ExternalInput").ap())
    out = nc.dram_tensor("out_0", (B, S, D), F32, kind="ExternalOutput").ap()
    build(nc, *args, out)
    r = _run(nc, [arrays], core_ids=[0])
    return r.results[0]["out_0"]
```

```python
from contextlib import ExitStack

import concourse.bass as bass
from concourse import mybir

F32 = mybir.dt.float32
F32R = mybir.dt.float32r
ACT = mybir.ActivationFunctionType
ALU = mybir.AluOpType
AX_X = mybir.AxisListType.X

P = 128
B = 4
S = 512
D = 512
KT = D // P
TT = S // P
H = 16
DH = 128
HG = 4
G = H // HG
MLP = 2048
JG = MLP // 512
NBLK = 8
PB = S // NBLK // TT
SCALE = float(DH) ** -0.5
EPS = 1e-6
HI, LO = 0, 1
MQ, MK, MV, MO = 0, 1, 2, 3
PAIRS = ((HI, HI), (HI, LO), (LO, HI))
SLOTS = B * HG


def group_order(first, last):
    steps = [("X", 0, k) for k in range(KT)] if first else []
    steps += [("K", 0, 0, KT), ("V", 0, 0), ("V", 0, 1), ("Q", 0, 0, KT), ("V", 0, 2), ("S", 0, 0), ("S", 0, 1),
              ("V", 0, 3), ("S", 0, 2), ("S", 0, 3)]
    for n in range(SLOTS):
        b, more = n // HG, n < SLOTS - 1
        xb = b + 1 if first and n % HG == 2 and b < B - 1 else n - SLOTS + 3 if last and n in (13, 14) else None
        x = [("X", xb, k) for k in range(KT)] if xb is not None else [None] * KT
        if more:
            steps += [("K", n + 1, 0, 4), ("C", n, 0), ("Q", n + 1, 0, 2), ("C", n, 1),
                      x[0], ("Q", n + 1, 2, 4), ("C", n, 2), x[1], ("C", n, 3)]
        else:
            steps += [("Y", b, 0, 0, 2), ("Y", b, 1, 0, 2), ("C", n, 0), ("C", n, 1), ("Y", b, 2, 0, 2)]
            steps += [("C", n, j) for j in range(2, TT)]
        if n % HG == 0 and n:
            steps += [("V", b, j) for j in range(TT)] + [("Y", b - 1, i, 0, HG) for i in range(TT)]
        d = [("D", n, j) for j in range(TT)]
        if more:
            steps += [x[2], d[0], ("S", n + 1, 0), ("S", n + 1, 1), d[1], x[3], d[2],
                      ("S", n + 1, 2), ("S", n + 1, 3), d[3]]
        else:
            steps += d
    steps += [("Y", b, i, 2, 3) for i in range(3)] + [("Y", b, i, 3, HG) for i in range(3)] + [("Y", b, 3, 0, HG)]
    return [s for s in steps if s is not None]


def mlp_order():
    def h(u):
        return [("H", u, j) for j in range(4)]

    def x(b):
        return [("X", b, k) for k in range(KT)]

    def z(u, i0=0, i1=TT):
        return [("Z", u, i) for i in range(i0, i1)]

    steps = h(0) + h(1) + z(0) + x(2)[:2] + z(1, 0, 1) + x(2)[2:] + z(1, 1, 3)
    steps += h(2) + z(1, 3, 4) + z(2, 0, 1) + x(3)[:2] + z(2, 1, 2) + x(3)[2:] + z(2, 2, 4) + h(3)
    for u in range(3, B * JG):
        steps += (h(u + 1) if u + 1 < B * JG else []) + z(u)
    return steps


def after(tiles, extra):
    out = []
    for t in tiles:
        out.append(t)
        out += extra.get(t, [])
    assert len(out) == len(tiles) + sum(map(len, extra.values()))
    return out


class Plan:

    def __init__(self, order):
        self.order = order
        self.done, started = [], []
        for s in order:
            whole = len(s) < 4 and s[0] != "D"
            tile = ("O", s[1]) if s[0] == "D" else s[:2] if s[0] in "KQ" else s[:3]
            if tile not in started:
                started.append(tile)
            end = {"K": KT, "Q": KT, "Y": HG}
            if whole or (s[2] == TT - 1 if s[0] == "D" else s[3 if s[0] in "KQ" else 4] == end[s[0]]):
                self.done.append(tile)
        m_tiles = [t for t in self.done if t[0] in "XKQVOYZ"]
        started = [t for t in started if t[0] in "XKQVOYZ"]
        self.at = {t: n for n, t in enumerate(m_tiles)}
        self.tiles = len(m_tiles)
        self.hi_at = {t: n for n, t in enumerate(t for t in m_tiles if t[0] not in "YZ")}
        self.his = len(self.hi_at)
        assert self.tiles % 4 == 0
        self.bank = {t: n % 4 for n, t in enumerate(started)}
        self.need = {t: self.at[started[n - 4]] + 1 for n, t in enumerate(started) if n >= 4}
        self.firsts = started[:4]
        self.tail = [self.at[t] + 1 - self.tiles for t in started[-4:]]

    def follow(self, tail):
        self.need.update(zip(self.firsts, tail))


FIRST, MIDDLE, LAST, MLP_PLAN = (Plan(group_order(True, False)), Plan(group_order(False, False)),
                                 Plan(group_order(False, True)), Plan(mlp_order()))
assert FIRST.tail == MIDDLE.tail == LAST.tail
for _plan in (MIDDLE, LAST, MLP_PLAN):
    _plan.follow(MIDDLE.tail)
NS = SLOTS * TT


def plan_of(g):
    return MIDDLE if not isinstance(g, int) else FIRST if g == 0 else LAST if g == G - 1 else MIDDLE


def m_base(g):
    return 0 if isinstance(g, int) and g == 0 else MIDDLE.tiles * g + (FIRST.tiles - MIDDLE.tiles)


def hi_base(g):
    return 0 if isinstance(g, int) and g == 0 else MIDDLE.his * g + (FIRST.his - MIDDLE.his)


M_MLP = m_base(G - 1) + LAST.tiles
HI_MLP = hi_base(G - 1) + LAST.his

FIRST_EXTRA = {}
for _b in range(1, B):
    _p = _b - 1
    for _i, _t in enumerate([("V", 0, 0), ("V", 0, 1), ("Q", 0), ("V", 0, 2)] if _p == 0 else
                            [("V", _p, _j) for _j in range(TT)]):
        FIRST_EXTRA[_t] = [("sum", _b, _i)]
    _n = HG * _p
    for _i, (_t, _m) in enumerate(
            [(("C", 0, 0), ("C", 0, 1)), (("C", 0, 3), ("S", 1, 1)), (("O", 0), ("C", 1, 0)),
             (("C", 1, 1), ("S", 2, 1))] if _p == 0 else
            [(("Y", _p - 1, 0),) * 2, (("Y", _p - 1, 2),) * 2, (("O", _n), ("C", _n + 1, 0)),
             (("C", _n + 1, 1), ("S", _n + 2, 1))]):
        FIRST_EXTRA.setdefault(_t, []).append(("aff", _b, _i))
        FIRST_EXTRA.setdefault(_m, []).append(("mom", _b, _i))
    for _i in range(TT):
        FIRST_EXTRA.setdefault(("O", HG * _p + 1), []).append(("hat", _b, _i))
LAST_EXTRA = {}
for _b in range(2):
    _n = HG * (_b + 1)
    for _i in range(TT):
        LAST_EXTRA[("O", _n + _i)] = [("res", _b, _i)]
        LAST_EXTRA.setdefault(("C", _n + HG, _i), []).append(("hat", _b, _i))
MLP_EXTRA = {}
for _i in range(TT):
    MLP_EXTRA[("H", 1, _i)] = [("res", 2, _i)]
    MLP_EXTRA[(("Z", 1, 0), ("Z", 1, 1), ("H", 2, 0), ("H", 2, 1))[_i]] = [("res", 3, _i)]
    MLP_EXTRA.setdefault(("Z", 0, 1 + _i // 2), []).append(("hat", 2, _i))
MLP_EXTRA[("Z", 1, 3)] = [("hat", 3, _i) for _i in range(TT)]


def build(nc, x, cond, rms_w, Wk, Wo, gamma, beta, ada_w, ada_b, qkv_w, qkv_b, out_w, out_b,
          ffn_w1, ffn_b1, ffn_w2, ffn_b2, out):
    ctx = ExitStack()
    with ctx:
        def sb(name, shape, dt=F32, stack=ctx):
            return stack.enter_context(nc.sbuf_tensor(name, shape, dt))

        def sem(name):
            return ctx.enter_context(nc.semaphore(name))

        x_mid = nc.dram_tensor("x_mid", (B, S, D), F32, kind="Internal").ap()
        xx_mid = nc.dram_tensor("xx_mid", (B, S, D), F32, kind="Internal").ap()
        xT_mid = [nc.dram_tensor(f"xT_mid{n}", (B, P, 2 * KT * S), F32, kind="Internal").ap() for n in range(2)]
        proj_mid = nc.dram_tensor("proj_mid", (B, D), F32, kind="Internal").ap()
        ada_mid = nc.dram_tensor("ada_mid", (B, 6 * D), F32, kind="Internal").ap()

        acc = sb("acc", [P, B * TT, D])
        W = sb("W", [P, 4, 2, 4, 512], F32R)
        raw = sb("raw", [P, 4, 512])
        prob = sb("prob", [P, TT, S])
        wide = sb("wide", [P, 2, D])
        proj = sb("proj", [P, D])
        ident = sb("ident", [P, P])
        cols = sb("cols", [P, 64])
        group_cols = sb("group_cols", [P, 12])
        ada_cols = sb("ada_cols", [P, 4, KT, B])
        neg_max = sb("neg_max", [P, TT])
        row_sum = sb("row_sum", [P, TT])
        row_inv = sb("row_inv", [P, TT])
        stats = sb("stats", [P, TT, 6])
        mean_var = sb("mean_var", [P, TT, 2])
        rstd = sb("rstd", [P, TT])
        minus_half = sb("minus_half", [P, TT])

        start = ExitStack()
        ada_raw = sb("ada_raw", [P, 4, KT, 512], stack=start)
        start.close()
        xT = sb("xT", [P, 2, 2, KT, S], F32R)
        start = ExitStack()
        WkT = sb("WkT", [P, KT, D], stack=start)
        WoT = sb("WoT", [P, KT, D], stack=start)
        raw2 = sb("raw2", [P, 4, 512], stack=start)
        Wk_sb = sb("Wk_sb", [P, KT, D], stack=start)
        ada = sb("ada", [B, 6 * D], stack=start)
        blocks = sb("blocks", [32, D], stack=start)
        blocksT = sb("blocksT", [P, KT, 32], stack=start)
        bias_rows = sb("bias_rows", [64, P], stack=start)
        small_row = sb("small_row", [1, 96], stack=start)
        block_ind = sb("block_ind", [P, 56], stack=start)
        ones = sb("ones", [1, P], stack=start)
        batch_mask = sb("batch_mask", [32, B], stack=start)
        condT = sb("condT", [P, KT, B], stack=start)
        small = sb("small", [32, 16], stack=start)
        Wo_sb = sb("Wo_sb", [P, KT, D], stack=start)
        start.close()
        proj_rows = Wk_sb[0:B, 0, :]
        att_sb = Wk_sb[:, 1, 0:KT * B]
        V = sb("V", [P, 2, TT, 512], F32R)
        probT = sb("probT", [P, 2, TT, S], F32R)
        later = ExitStack()
        O = sb("O", [P, 2, HG, S], F32R, stack=later)
        later.close()
        xx_in = sb("xx_in", [P, 2, TT, D])
        QK = sb("QK", [P, 2, 2, S], F32R)
        hid = [V, probT]
        cond_sb = proj[0:B, :]

        ps_s = ctx.enter_context(nc.psum_tensor("ps_s", [P, 2, 512], F32))
        ps_c = ctx.enter_context(nc.psum_tensor("ps_c", [P, 2, 512], F32))
        ps_m = ctx.enter_context(nc.psum_tensor("ps_m", [P, 4, 512], F32))
        adaT_bank = [ps_m[:, 3, :], ps_c[:, 0, :]]
        four = [ps_s[:, 0, :], ps_s[:, 1, :], ps_c[:, 0, :], ps_c[:, 1, :]]

        def f(ap):
            return ap.bitcast(F32)

        x_loaded = [sem(f"x_loaded{b}") for b in range(B)]
        small_loaded = sem("small_loaded")
        rq_loaded = sem("rq_loaded")
        affine_loaded = sem("affine_loaded")
        adab_loaded = sem("adab_loaded")
        wk_loaded = sem("wk_loaded")
        wo_loaded = sem("wo_loaded")
        adaw_loaded = [sem(f"adaw_loaded{n}") for n in range(6)]
        consts = sem("consts")
        const_step = sem("const_step")
        dve_step = sem("dve_step")
        pro_cols = sem("pro_cols")
        pro_condT = sem("pro_condT")
        token_sums = sem("token_sums")
        pro_blocks = sem("pro_blocks")
        pro_blocks_sb = sem("pro_blocks_sb")
        pro_blocksT = sem("pro_blocksT")
        pro_blocksT_sb = sem("pro_blocksT_sb")
        wT_psum = sem("wT_psum")
        wT_sb = sem("wT_sb")
        pro_keys = sem("pro_keys")
        keys_sb = sem("keys_sb")
        keys_sq = sem("keys_sq")
        keys_mean = sem("keys_mean")
        keys_rms = sem("keys_rms")
        score_col = sem("score_col")
        score_row = sem("score_row")
        score_exp_in = sem("score_exp_in")
        score_exp = sem("score_exp")
        attn_row = sem("attn_row")
        attn_col = sem("attn_col")
        attn_mask = sem("attn_mask")
        att_psum = sem("att_psum")
        att_copied = sem("att_copied")
        proj_psum = sem("proj_psum")
        proj_sb = sem("proj_sb")
        proj_bc = sem("proj_bc")
        proj_stored = sem("proj_stored")
        proj_loaded = sem("proj_loaded")
        ada_psum = sem("ada_psum")
        ada_sb = sem("ada_sb")
        adaT_psum = sem("adaT_psum")
        ada_cols_sb = sem("ada_cols_sb")
        ada_stored = sem("ada_stored")
        sum_done = sem("sum_done")
        xb_done = sem("xb_done")
        var_ready = sem("var_ready")
        var_eps = sem("var_eps")
        rstd_ready = sem("rstd_ready")
        x_new = sem("x_new")
        x_stored = sem("x_stored")
        hat_done = sem("hat_done")
        x_mod = sem("x_mod")
        xT_stored = [sem(f"xT_stored{n}") for n in range(2)]
        xT_loaded = [sem(f"xT_loaded{n}") for n in range(2)]
        acc_init = [sem(f"acc_init{b}") for b in range(B)]
        raw_loaded = sem("raw_loaded")
        raw_free = sem("raw_free")
        w_scaled = sem("w_scaled")
        w_hi = sem("w_hi")
        w_split = sem("w_split")
        m_done = sem("m_done")
        m_free = sem("m_free")
        hi_done = sem("hi_done")
        s_done = sem("s_done")
        max_done = sem("max_done")
        exp_done = sem("exp_done")
        inv_done = sem("inv_done")
        norm_done = sem("norm_done")
        c_done = sem("c_done")
        c_hi = sem("c_hi")
        c_lo = sem("c_lo")
        pool_waited = sem("pool_waited")
        sp_waited = sem("sp_waited")
        group_cols_set = sem("group_cols_set")
        wide_loaded = [sem(f"wide_loaded{n}") for n in range(2)]
        x_back = sem("x_back")
        res_done = sem("res_done")
        xx_done = sem("xx_done")
        xx_stored = sem("xx_stored")
        h_done = sem("h_done")
        gelu_done = sem("gelu_done")
        h_hi = sem("h_hi")
        h_lo = sem("h_lo")
        xx_loaded = [sem(f"xx_loaded{n}") for n in range(2)]
        fin_done = sem("fin_done")
        out_stored = sem("out_stored")

        def rows(ap, b):
            return ap[b].rearrange("(p i) d -> p i d", i=TT)

        ada_v = ada_w.rearrange("(k p) (c n) -> c p k n", p=P, n=512)
        qkv_v = qkv_w.rearrange("(k p) (m g c) -> m g p k c", p=P, m=3, g=G)
        ow_v = out_w.rearrange("(g h p) n -> g p h n", g=G, p=P)
        w1_v = ffn_w1.rearrange("(k p) (g c) -> g p k c", p=P, g=JG)
        w2_v = ffn_w2.rearrange("(g h p) n -> g p h n", g=JG, p=P)

        def bcast(row, parts):
            return row.rearrange("(a n) -> a n", a=1).partition_broadcast(parts)

        def pick(view, g):
            if isinstance(g, int):
                return view[g]
            return view[bass.ds(g, 1)].rearrange("a p k c -> (a p) k c")

        def xT_tile(n):
            return f(xT[:, n].rearrange("p s k t -> p (s k t)"))

        def tiles(b):
            return slice(TT * b, TT * b + TT)

        FFN_AT = [(MV, MQ), (MK, MO), (MV, MQ), (MK, MO)]
        R_MLP = 4 * G
        ada_buf = [ada_raw[:, n] for n in range(4)] + [Wo_sb, WkT]

        def hat_tile(stage, b, i):
            if stage:
                return acc[:, TT * b + i, :]
            return (prob if b == 0 else raw)[:, i, :]

        block = ctx.enter_context(nc.Block())

        @block.sync
        def _(sp):
            def store_xT(n, b, m):
                sp.wait_ge(m_free, m)
                sp.dma_start(xT_mid[n][b], xT_tile(b % 2)).then_inc(xT_stored[b % 2], 16)

            def load_xT(src, b):
                sp.dma_start(xT_tile(b % 2), src[b]).then_inc(xT_loaded[b % 2], 16)

            def load_raw(src, g, r):
                sp.wait_ge(raw_free, r)
                sp.sem_inc(sp_waited, 1)
                sp.dma_start(raw[:, :, :], pick(src, g)).then_inc(raw_loaded, 16)

            def init_acc(b, row):
                for i in range(TT):
                    sp.dma_start(acc[:, TT * b + i, :], bcast(row, P)).then_inc(acc_init[b], 16)

            sp.dma_start(cond_sb, cond).then_inc(small_loaded, 16)
            sp.dma_start(bias_rows[0:48, :], qkv_b.rearrange("(r c) -> r c", c=P)).then_inc(small_loaded, 16)
            sp.dma_start(bias_rows[48:64, :], ffn_b1.rearrange("(r c) -> r c", c=P)).then_inc(small_loaded, 16)
            for b in range(B):
                sp.dma_start(acc[:, tiles(b), :], rows(x, b)).then_inc(x_loaded[b], 16)
            sp.dma_start(Wk_sb[:, :, :], Wk.rearrange("(r p) h -> p r h", p=P)).then_inc(wk_loaded, 16)
            sp.dma_start(prob[0:32, 0, :], bcast(rms_w, 32)).then_inc(rq_loaded, 16)
            sp.dma_start(prob[0:32, 1, :], bcast(cond[1], 32)).then_inc(rq_loaded, 16)
            sp.dma_start(Wo_sb[:, :, :], Wo.rearrange("(r p) h -> p r h", p=P)).then_inc(wo_loaded, 16)
            sp.dma_start(raw[:, :, :], pick(qkv_v[MV], 0)).then_inc(raw_loaded, 16)
            sp.dma_start(wide[:, 0, :], bcast(gamma, P)).then_inc(affine_loaded, 16)
            sp.dma_start(wide[:, 1, :], bcast(beta, P)).then_inc(affine_loaded, 16)
            sp.dma_start(ada[:, :], bcast(ada_b, B)).then_inc(adab_loaded, 16)
            for c in range(2):
                sp.dma_start(ada_buf[c], ada_v[c]).then_inc(adaw_loaded[c], 16)
            sp.wait_ge(raw_loaded, 16)
            sp.wait_ge(pro_blocks, 1)
            sp.dma_start(raw2[:, :, :], pick(qkv_v[MK], 0)).then_inc(raw_loaded, 16)
            sp.wait_ge(wT_psum, 2 * KT)
            sp.wait_ge(pro_keys, 1)
            for c in range(2, 6):
                if c == 4:
                    sp.wait_ge(raw_free, 1)
                    sp.wait_ge(raw_loaded, 32)
                    sp.dma_start(raw[:, :, :], pick(qkv_v[MQ], 0)).then_inc(raw_loaded, 16)
                sp.dma_start(ada_buf[c][:, :, :], ada_v[c]).then_inc(adaw_loaded[c], 16)
            def load_proj(b):
                sp.dma_start(proj[:, :], bcast(proj_mid[b], P)).then_inc(proj_loaded, 16)

            sp.wait_ge(proj_sb, 1)
            sp.dma_start(proj_mid, proj_rows).then_inc(proj_stored, 16)
            sp.wait_ge(proj_stored, 16)
            load_proj(1)
            sp.wait_ge(raw_free, 2)
            sp.wait_ge(raw_loaded, 48)
            sp.dma_start(raw2[:, :, :], pick(ow_v, 0)).then_inc(raw_loaded, 16)
            for b in range(B):
                sp.wait_ge(x_new, b + 1)
                if b in (1, 2):
                    load_proj(b + 1)
                sp.dma_start(rows(x_mid, b), acc[:, tiles(b), :]).then_inc(x_stored, 16)
                store_xT(0, b, FIRST.at[("X", b, KT - 1)] + 1)
                if b == 0:
                    sp.wait_ge(ada_sb, 6)
                    sp.dma_start(ada_mid, ada[:, :]).then_inc(ada_stored, 16)
                sp.wait_ge(x_stored, 16 * (b + 1))
                sp.wait_ge(hat_done, TT * (b + 1))
                init_acc(b, out_b)
            for n in range(2):
                sp.wait_ge(xT_stored[n], 32)

            def group(g):
                plan, base = plan_of(g), m_base(g)
                last = plan is LAST

                def used(b):
                    sp.wait_ge(m_done, base + plan.at[("Q", HG * b + 3)] + 1)
                    sp.sem_inc(sp_waited, 1)

                if plan is not FIRST:
                    load_raw(ow_v, g, 4 * g + 3)
                    used(0)
                    load_xT(xT_mid[0], 2)
                if last:
                    sp.wait_ge(ada_stored, 16)
                    for b in range(2):
                        sp.dma_start(wide[:, b, :], bcast(ada_mid[b, 2 * D:3 * D], P)).then_inc(wide_loaded[b], 16)
                    sp.wait_ge(raw_free, 4 * g + 4)
                    sp.dma_start(raw[:, :, :], rows(x_mid, 0)).then_inc(x_back, 16)
                    used(1)
                    load_xT(xT_mid[0], 3)
                    store_xx(0)
                    sp.dma_start(raw[:, :, :], rows(x_mid, 1)).then_inc(x_back, 16)
                    load_gate(2, 2)
                    store_xx(1)
                    load_raw(w1_v, 0, R_MLP)
                    load_gate(3, 2)
                    load_raw(w2_v, 0, R_MLP + 1)
                    return
                if plan is not FIRST:
                    load_raw(qkv_v[MV], g + 1, 4 * g + 4)
                    used(1)
                    load_xT(xT_mid[0], 3)
                    used(2)
                    load_xT(xT_mid[0], 0)
                else:
                    load_xT(xT_mid[0], 0)
                    load_raw(qkv_v[MV], g + 1, 4 * g + 4)
                load_raw(qkv_v[MK], g + 1, 4 * g + 5)
                used(3)
                load_xT(xT_mid[0], 1)
                load_raw(qkv_v[MQ], g + 1, 4 * g + 6)

            def store_xx(b):
                sp.wait_ge(xx_done, TT * (b + 1))
                sp.dma_start(rows(xx_mid, b), raw[:, :, :]).then_inc(xx_stored, 16)
                sp.wait_ge(xx_stored, 16 * (b + 1))

            def load_gate(b, part):
                if part == 2:
                    sp.wait_ge(res_done, TT * (b - 1))
                elif b < 2:
                    sp.wait_ge(res_done, TT * B)
                else:
                    sp.wait_ge(fin_done, TT * (b - 1))
                sp.dma_start(wide[:, b % 2, :], bcast(ada_mid[b, part * D:(part + 1) * D], P)) \
                    .then_inc(wide_loaded[b % 2], 16)

            group(0)
            with sp.Fori(1, G - 1) as g:
                group(g)
            group(G - 1)
            for b in range(2):
                store_xT(1, b, m_base(G - 1) + LAST.at[("X", b, KT - 1)] + 1)
                init_acc(b, ffn_b2)
                if b == 0:
                    sp.wait_ge(raw_free, R_MLP + 2)
                    sp.dma_start(raw[:, :, :], rows(x_mid, 2)).then_inc(x_back, 16)
            store_xx(2)
            sp.dma_start(raw[:, :, :], rows(x_mid, 3)).then_inc(x_back, 16)
            store_xT(1, 2, M_MLP + MLP_PLAN.at[("X", 2, KT - 1)] + 1)
            init_acc(2, ffn_b2)
            store_xx(3)
            load_raw(w1_v, 1, R_MLP + 2)
            sp.wait_ge(xT_stored[0], 64)
            sp.wait_ge(h_done, 4 * (B - 1))
            load_xT(xT_mid[1], 0)
            store_xT(1, 3, M_MLP + MLP_PLAN.at[("X", 3, KT - 1)] + 1)
            init_acc(3, ffn_b2)
            sp.wait_ge(xT_stored[1], 64)
            for b in range(2):
                load_gate(b, 5)
            sp.wait_ge(xx_stored, 16 * B)
            for u in range(B, B * JG):
                if u > B:
                    sp.wait_ge(h_done, 4 * (u - 1))
                    load_xT(xT_mid[1], u % B)
                jg = u // B + 1
                if u == B + 1:
                    load_raw(w2_v, 1, R_MLP + 3)
                if jg < JG and u % B == 2:
                    load_raw(w1_v, jg, R_MLP + 2 * jg)
                if jg < JG and u % B == 3:
                    load_raw(w2_v, jg, R_MLP + 2 * jg + 1)
                if u in (B, B + 1):
                    sp.dma_start(xx_in[:, u % B, :, :], rows(xx_mid, u % B)).then_inc(xx_loaded[u % B], 16)
            for b in range(B):
                for i in range(TT):
                    sp.wait_ge(fin_done, TT * b + i + 1)
                    sp.dma_start(rows(out, b)[:, i, :], acc[:, TT * b + i, :]).then_inc(out_stored, 16)
                if b < 2:
                    load_gate(b + 2, 5)
                    sp.dma_start(xx_in[:, b, :, :], rows(xx_mid, b + 2)).then_inc(xx_loaded[b], 16)
            sp.wait_ge(out_stored, 16 * B * TT)

        def piece(mat, q):
            return (lambda t: t[:, :, P * q:P * q + P]) if mat in (MQ, MK) else (lambda t: t[:, q, :])

        @block.gpsimd
        def _(pool):
            step = [0]

            def link(ins):
                step[0] += 1
                ins.then_inc(const_step, 1)
                pool.wait_ge(const_step, step[0])

            def hold(semaphore, value):
                pool.wait_ge(semaphore, value)
                pool.sem_inc(pool_waited, 1)

            link(nc.gpsimd.memset(ident[:, :], 0.0))
            link(nc.gpsimd.affine_select(out=ident[:, :], in_=ident[:, :], compare_op=ALU.not_equal, fill=1.0,
                                         base=0, pattern=[[-1, P]], channel_multiplier=1))
            link(nc.gpsimd.memset(block_ind[:, :], 1.0))
            link(nc.gpsimd.affine_select(out=block_ind[:, :], in_=block_ind[:, :], compare_op=ALU.is_ge, fill=0.0,
                                         base=PB * (B - 1) * NBLK, pattern=[[-PB, 56]], channel_multiplier=1))
            link(nc.gpsimd.affine_select(out=block_ind[:, :], in_=block_ind[:, :], compare_op=ALU.is_ge, fill=0.0,
                                         base=PB - 1 - PB * (B - 1) * NBLK, pattern=[[PB, 56]],
                                         channel_multiplier=-1))
            link(nc.gpsimd.memset(batch_mask[:, :], 1.0))
            link(nc.gpsimd.affine_select(out=batch_mask[:, :], in_=batch_mask[:, :], compare_op=ALU.is_ge, fill=0.0,
                                         base=0, pattern=[[-NBLK, B]], channel_multiplier=1))
            link(nc.gpsimd.affine_select(out=batch_mask[:, :], in_=batch_mask[:, :], compare_op=ALU.is_ge, fill=0.0,
                                         base=NBLK - 1, pattern=[[NBLK, B]], channel_multiplier=-1))
            link(nc.gpsimd.memset(minus_half[:, :], -0.5))
            nc.gpsimd.memset(ones[:, :], 1.0).then_inc(consts, 1)

            def split(mat, dst, q, r, scale, src_of):
                at = piece(mat, q)
                src, hi, lo = at(src_of), at(W[:, dst, HI]), at(W[:, dst, LO])
                if scale != 1.0:
                    nc.gpsimd.tensor_scalar(src, src, scale, 1.0, ALU.mult, ALU.mult).then_inc(w_scaled, 1)
                    hold(w_scaled, r - 2 + q + 1)
                nc.gpsimd.tensor_scalar(hi, src, 1.0, 1.0, ALU.mult, ALU.mult).then_inc(w_hi, 1)
                hold(w_hi, 4 * r + q + 1)
                nc.gpsimd.tensor_tensor(lo, src, f(hi), ALU.subtract).then_inc(w_split, 1)

            def split_pieces(mat, dst, r, pieces=range(4), scale=1.0, wait=None, src=raw):
                for q in pieces:
                    if q == 0:
                        hold(raw_loaded, 16 * (r + 1))
                    if wait is not None:
                        wait(q)
                    split(mat, dst, q, r, scale, src)
                    if q == 3:
                        hold(w_split, 4 * (r + 1))
                        pool.sem_inc(raw_free, 1)

            def inverse_std(call):
                pool.wait_ge(var_ready, call + 1)
                nc.gpsimd.tensor_scalar(rstd[:, :], mean_var[:, :, 1], 1.0, EPS, ALU.mult, ALU.add).then_inc(var_eps, 1)
                pool.wait_ge(var_eps, call + 1)
                nc.gpsimd.tensor_tensor(rstd[:, :], rstd[:, :], minus_half[:, :], ALU.pow).then_inc(rstd_ready, 1)

            def add_beta(b):
                for i in range(TT):
                    pool.wait_ge(sum_done, TT * b + i + 1)
                    nc.gpsimd.tensor_tensor(acc[:, TT * b + i, :], acc[:, TT * b + i, :], wide[:, 1, :],
                                            ALU.add).then_inc(xb_done, 1)

            def add_xx(b, parts=range(TT)):
                pool.wait_ge(x_back, 16 * (b + 1))
                for i in parts:
                    pool.wait_ge(res_done, TT * b + i + 1)
                    nc.gpsimd.tensor_tensor(raw[:, i, :], raw[:, i, :], acc[:, TT * b + i, :],
                                            ALU.add).then_inc(xx_done, 1)

            split_pieces(MV, MV, 0, range(0, 3))
            pool.wait_ge(keys_mean, 1)
            nc.gpsimd.tensor_tensor(small[:, 3:4], small[:, 1:2], minus_half[0:32, 0:1], ALU.pow).then_inc(keys_rms, 1)
            split_pieces(MV, MV, 0, range(3, 4))
            split_pieces(MK, MK, 1, src=raw2)
            split_pieces(MQ, MQ, 2, range(0, 1), scale=SCALE)
            pool.wait_ge(affine_loaded, 32)
            add_beta(0)
            inverse_std(0)
            split_pieces(MQ, MQ, 2, range(1, 4), scale=SCALE)
            inverse_std(1)
            split_pieces(MO, MO, 3, src=raw2)

            def normalise(g, n):
                for t in range(TT):
                    hold(inv_done, NS * g + TT * n + t + 1)
                    nc.gpsimd.tensor_scalar(prob[:, t, :], prob[:, t, :], row_inv[:, t:t + 1], 1.0,
                                            ALU.mult, ALU.mult).then_inc(norm_done, 1)

            def group(g):
                plan, base = plan_of(g), m_base(g)
                last = plan is LAST

                def used(tile):
                    return lambda q: hold(m_done, base + plan.at[tile] + 1)

                def head_used(q):
                    hold(m_done, base + plan.at[("Q", 12 + q)] + 1)

                for n in range(SLOTS):
                    if n == 13 and not last:
                        split_pieces(MV, MV, 4 * g + 4, wait=used(("V", 3, 3)))
                    if n in (13, 14) and last:
                        split_pieces(MQ, MV, 4 * g + 4, range(2) if n == 13 else range(2, 4),
                                     wait=used(("V", 3, 3)))
                    if n == 14 and not last:
                        split_pieces(MK, MK, 4 * g + 5, range(0, 2), wait=head_used)
                    if n == 15 and not last:
                        split_pieces(MK, MK, 4 * g + 5, range(2, 3), wait=head_used)
                    normalise(g, n)
                    if plan is FIRST:
                        if n == 0:
                            inverse_std(2)
                            add_beta(1)
                        if n in (4, 8):
                            add_beta(n // HG + 1)
                            inverse_std(2 * (n // HG) + 2)
                        if n in (1, 5, 9):
                            inverse_std(2 * (n // HG) + 3)
                    elif n == 2:
                        split_pieces(MO, MO, 4 * g + 3, wait=lambda q: hold(m_done, base + 1))
                    if last and HG < n <= 3 * HG:
                        b, i = divmod(n - HG - 1, TT)
                        if i == TT - 1:
                            inverse_std(2 * B + b)
                        add_xx(b, range(i, i + 1))
                if last:
                    split_pieces(MO, MQ, 4 * g + 5, wait=lambda q: head_used(3))
                else:
                    split_pieces(MK, MK, 4 * g + 5, range(3, 4), wait=head_used)
                    split_pieces(MQ, MQ, 4 * g + 6, scale=SCALE, wait=head_used)

            group(0)
            with pool.Fori(1, G - 1) as g:
                group(g)
            group(G - 1)
            for b in (2, 3):
                add_xx(b)
                inverse_std(2 * B + b)
            for jg in range(1, JG):
                split_pieces(MQ, FFN_AT[jg][0], R_MLP + 2 * jg,
                             wait=lambda q: pool.wait_ge(h_done, 4 * B * (jg - 1)) if jg > 1 else None)
                split_pieces(MO, FFN_AT[jg][1], R_MLP + 2 * jg + 1,
                             wait=lambda q: pool.wait_ge(m_done, M_MLP + MLP_PLAN.at[("Z", B * jg - B - 1, TT - 1)] + 1
                                                         if jg > 1 else M_MLP))

        @block.scalar
        def _(act):
            for m in range(2):
                for k in range(KT):
                    act.wait_ge(wT_psum, KT * m + k + 1)
                    nc.scalar.copy((WkT, WoT)[m][:, k, :], four[k]).then_inc(wT_sb, 1)
            act.wait_ge(keys_sb, 1)
            nc.scalar.activation(prob[0:32, 3, :], prob[0:32, 2, :], ACT.Square,
                                 accum_out=small[:, 0:1]).then_inc(keys_sq, 1)
            act.wait_ge(score_exp_in, 1)
            nc.scalar.activation(small_row[:, 32:64], small_row[:, 32:64], ACT.Exp).then_inc(score_exp, 1)
            act.wait_ge(proj_psum, 1)
            nc.scalar.copy(proj_rows, ps_m[0:B, 2, :]).then_inc(proj_sb, 1)

            def hi(dst, bank, bias):
                if bias is None:
                    nc.scalar.copy(dst, bank).then_inc(hi_done, 1)
                else:
                    nc.scalar.activation(dst, bank, ACT.Identity, bias=bias).then_inc(hi_done, 1)

            mods = [0]

            def modulate(stage, b, k, bank):
                if b >= 2 or stage:
                    act.wait_ge(xT_stored[b % 2], 16 * (b // 2 + 2 * stage))
                mods[0] += 1
                nc.scalar.activation(bank, bank, ACT.Identity, bias=ada_cols[:, 2 * stage, k, b:b + 1],
                                     scale=ada_cols[:, 2 * stage + 1, k, b:b + 1]).then_inc(x_mod, 1)
                act.wait_ge(x_mod, mods[0])
                hi(xT[:, b % 2, HI, k, :], bank, None)

            def group(g):
                plan, base = plan_of(g), m_base(g)
                if plan is not FIRST:
                    act.wait_ge(group_cols_set, g + 1)
                for tile in plan.done:
                    kind, n = tile[0], tile[1]
                    if tile in plan.hi_at:
                        act.wait_ge(m_done, base + plan.at[tile] + 1)
                    bank = ps_m[:, plan.bank[tile], :] if tile in plan.at else None
                    h = n % HG
                    if tile == ("K", 0) and plan is FIRST:
                        act.wait_ge(group_cols_set, 1)
                    if kind == "X":
                        if plan is FIRST and n == 0 and tile[2] == 0:
                            act.wait_ge(ada_cols_sb, 2)
                        modulate(0 if plan is FIRST else 1, n, tile[2], bank)
                    elif kind == "K":
                        hi(QK[:, 1, HI, :], bank, group_cols[:, HG + h:HG + h + 1])
                    elif kind == "Q":
                        hi(QK[:, 0, HI, :], bank, group_cols[:, h:h + 1])
                    elif kind == "V":
                        hi(V[:, HI, tile[2], :], bank, None)
                    elif kind == "O":
                        if plan is FIRST and n == 0:
                            act.wait_ge(ada_stored, 16)
                        hi(O[:, HI, h, :], bank, group_cols[:, 2 * HG + h:2 * HG + h + 1])
                    elif kind == "S":
                        t = tile[2]
                        act.wait_ge(max_done, NS * g + TT * n + t + 1)
                        nc.scalar.activation(prob[:, t, :], ps_s[:, (TT * n + t) % 2, :], ACT.Exp,
                                             bias=neg_max[:, t:t + 1],
                                             accum_out=row_sum[:, t:t + 1]).then_inc(exp_done, 1)
                    elif kind == "C":
                        j = tile[2]
                        act.wait_ge(c_done, NS * g + TT * n + j + 1)
                        nc.scalar.copy(probT[:, HI, j, :], ps_c[:, (TT * n + j) % 2, :]).then_inc(c_hi, 1)

            group(0)
            with act.Fori(1, G - 1) as g:
                group(g)
            group(G - 1)
            for tile in MLP_PLAN.done:
                kind, u = tile[0], tile[1]
                if kind == "X":
                    act.wait_ge(m_done, M_MLP + MLP_PLAN.at[tile] + 1)
                    modulate(1, u, tile[2], ps_m[:, MLP_PLAN.bank[tile], :])
                elif kind == "H":
                    j = tile[2]
                    n = 4 * u + j
                    act.wait_ge(h_done, n + 1)
                    if n >= 4:
                        act.wait_ge(h_lo, n - 3)
                    nc.scalar.activation(prob[:, j, :], four[j], ACT.Gelu,
                                         bias=cols[:, 3 * H + 4 * (u // B) + j:3 * H + 4 * (u // B) + j + 1]) \
                        .then_inc(gelu_done, 1)

        @block.vector
        def _(dve):
            count = [0]

            def link(ins):
                count[0] += 1
                ins.then_inc(dve_step, 1)
                dve.wait_ge(dve_step, count[0])

            v = nc.vector
            dve.wait_ge(pro_cols, 1)
            link(v.tensor_copy(cols[:, :], ps_m[:, 0, 0:64]))
            link(v.tensor_scalar(cols[:, 0:H], cols[:, 0:H], SCALE, None, ALU.mult))
            v.tensor_copy(condT[:, :, :], ps_m[:, 1, 0:16].rearrange("p (k b) -> p k b", b=B)).then_inc(pro_condT, 1)
            for b in range(B):
                dve.wait_ge(x_loaded[b], 16)
                v.tensor_reduce(raw2[:, b, :], acc[:, tiles(b), :].rearrange("p i d -> p d i"), axis=AX_X,
                                op=ALU.add).then_inc(token_sums, 1)
            dve.wait_ge(pro_blocks, 1)
            v.tensor_copy(blocks[:, :], ps_m[0:32, 2, :]).then_inc(pro_blocks_sb, 1)
            dve.wait_ge(pro_blocksT, 1)
            v.tensor_copy(blocksT[:, :, :], ps_m[:, 3, 0:128].rearrange("p (k n) -> p k n", n=32)) \
                .then_inc(pro_blocksT_sb, 1)
            dve.wait_ge(rq_loaded, 32)
            link(v.tensor_tensor(prob[0:32, 1, :], prob[0:32, 1, :], prob[0:32, 0, :], ALU.mult))
            dve.wait_ge(pro_keys, 1)
            v.tensor_copy(prob[0:32, 2, :], ps_m[0:32, 0, :]).then_inc(keys_sb, 1)
            dve.wait_ge(keys_sb, 1)
            link(v.tensor_tensor(prob[0:32, 0, :], prob[0:32, 1, :], prob[0:32, 2, :], ALU.mult))
            link(v.reduce_sum(small[:, 2:3], prob[0:32, 0, :], axis=AX_X))
            dve.wait_ge(keys_sq, 1)
            v.tensor_scalar(small[:, 1:2], small[:, 0:1], 1.0 / D, EPS, ALU.mult, ALU.add).then_inc(keys_mean, 1)
            dve.wait_ge(keys_rms, 1)
            v.tensor_tensor(small[:, 4:5], small[:, 2:3], small[:, 3:4], ALU.mult).then_inc(score_col, 1)
            dve.wait_ge(score_row, 1)
            r = small_row
            scores = ps_m[0:1, 1, 64:96].rearrange("p (b n) -> p b n", n=NBLK)
            expd = r[:, 32:64].rearrange("p (b n) -> p b n", n=NBLK)
            link(v.tensor_reduce(r[:, 0:4], scores, axis=AX_X, op=ALU.max))
            v.tensor_tensor(expd, scores, r[:, 0:4].unsqueeze(2).to_broadcast([1, B, NBLK]),
                            ALU.subtract).then_inc(score_exp_in, 1)
            dve.wait_ge(score_exp, 1)
            link(v.reduce_sum(r[:, 4:8], expd, axis=AX_X))
            link(v.reciprocal(r[:, 8:12], r[:, 4:8]))
            v.tensor_tensor(r[:, 64:96].rearrange("p (b n) -> p b n", n=NBLK), expd,
                            r[:, 8:12].unsqueeze(2).to_broadcast([1, B, NBLK]), ALU.mult).then_inc(attn_row, 1)
            dve.wait_ge(attn_col, 1)
            link(v.tensor_copy(small[:, 5:6], ps_m[0:32, 1, 100:101]))
            v.tensor_scalar(small[:, 8:12], batch_mask[:, :], small[:, 5:6], None, ALU.mult).then_inc(attn_mask, 1)
            dve.wait_ge(att_psum, 1)
            dve.wait_ge(wT_psum, KT)
            v.tensor_copy(att_sb, ps_m[:, 1, 128:144]).then_inc(att_copied, 1)

            def add_ada(c):
                dve.wait_ge(ada_psum, c + 1)
                v.tensor_tensor(ada[:, 512 * c:512 * c + 512], ada[:, 512 * c:512 * c + 512],
                                four[c % 4][0:B, :], ALU.add).then_inc(ada_sb, 1)

            def ada_columns(half):
                dve.wait_ge(adaT_psum, half + 1)
                link(v.tensor_copy(ada_cols[:, 2 * half:2 * half + 2],
                                   adaT_bank[half][:, 0:32].rearrange("p (y k b) -> p y k b", y=2, k=KT)))
                v.tensor_scalar(ada_cols[:, 2 * half + 1], ada_cols[:, 2 * half + 1], 1.0, None,
                                ALU.add).then_inc(ada_cols_sb, 2 - half)

            def moments(src, i):
                link(v.bn_stats(stats[:, i, :], src))
                last = v.bn_aggr(mean_var[:, i, :], stats[:, i, :])
                if i < TT - 1:
                    link(last)
                else:
                    last.then_inc(var_ready, 1)

            def norm_step(stage, tile):
                kind, b, i = tile
                z, a = hat_tile(stage, b, i), acc[:, TT * b + i, :]
                mean, inv = mean_var[:, i, 0:1], rstd[:, i:i + 1]
                if kind == "sum":
                    if b == 0:
                        dve.wait_ge(proj_bc, 1)
                        src = ps_m[:, 0, :]
                    else:
                        if i == 0:
                            dve.wait_ge(proj_loaded, 16 * b)
                            if b == 1:
                                dve.wait_ge(raw_free, 3)
                            else:
                                dve.wait_ge(m_done, FIRST.at[("X", b - 1, KT - 1)] + 1)
                        src = proj[:, :]
                    v.tensor_tensor(z, a, src, ALU.add).then_inc(sum_done, 1)
                    dve.wait_ge(sum_done, TT * b + i + 1)
                    moments(z, i)
                elif kind == "aff":
                    if i == 0:
                        dve.wait_ge(rstd_ready, 2 * b + 1)
                        dve.wait_ge(affine_loaded, 32)
                    link(v.scalar_tensor_tensor(out=z, in0=z, scalar=mean, in1=wide[:, 0, :],
                                                op0=ALU.subtract, op1=ALU.mult))
                    dve.wait_ge(xb_done, TT * b + i + 1)
                    link(v.scalar_tensor_tensor(out=a, in0=z, scalar=inv, in1=a, op0=ALU.mult, op1=ALU.add))
                    if i == TT - 1:
                        dve.sem_inc(x_new, 1)
                elif kind == "mom":
                    moments(a, i)
                elif kind == "res":
                    if i == 0:
                        dve.wait_ge(wide_loaded[b % 2], 16 * (b // 2 + 1))
                        dve.wait_ge(x_back, 16 * (b + 1))
                    link(v.tensor_tensor(a, a, wide[:, b % 2, :], ALU.mult))
                    v.tensor_tensor(a, a, raw[:, i, :], ALU.add).then_inc(res_done, 1)
                    dve.wait_ge(res_done, TT * b + i + 1)
                    moments(a, i)
                else:
                    if i == 0:
                        dve.wait_ge(rstd_ready, 2 * B + b + 1 if stage else 2 * b + 2)
                    if stage:
                        dve.wait_ge(xx_done, TT * b + i + 1)
                    v.tensor_scalar(z, a, mean, inv, ALU.subtract, ALU.mult).then_inc(hat_done, 1)

            dve.wait_ge(adab_loaded, 16)
            for kind in ("sum", "aff", "hat"):
                for i in range(TT):
                    norm_step(0, (kind, 0, i))
                    if kind == "aff":
                        norm_step(0, ("mom", 0, i))
                if kind == "sum":
                    add_ada(0)
                    add_ada(1)
                elif kind == "aff":
                    ada_columns(0)

            def inverse(g, s):
                dve.wait_ge(exp_done, NS * g + s + 1)
                v.reciprocal(row_inv[:, s % TT:s % TT + 1], row_sum[:, s % TT:s % TT + 1]).then_inc(inv_done, 1)

            def lo(dst, hi_part, bank, bias):
                if bias is None:
                    v.tensor_tensor(dst, bank, f(hi_part), ALU.subtract).then_inc(m_free, 1)
                else:
                    v.scalar_tensor_tensor(out=dst, in0=bank, scalar=bias, in1=f(hi_part), op0=ALU.add,
                                           op1=ALU.subtract).then_inc(m_free, 1)

            def set_group_cols(g):
                at = slice(0, HG) if isinstance(g, int) and g == 0 else bass.ds(HG * g, HG)
                v.tensor_copy(group_cols[:, :].rearrange("p (m h) -> p m h", m=3),
                              cols[:, 0:3 * H].rearrange("p (m h) -> p m h", m=3)[:, :, at]) \
                    .then_inc(group_cols_set, 1)
                dve.wait_ge(group_cols_set, g + 1)

            def group(g):
                plan, base, his = plan_of(g), m_base(g), hi_base(g)
                extra = {FIRST: FIRST_EXTRA, LAST: LAST_EXTRA}.get(plan, {})
                set_group_cols(g)
                for tile in after(plan.done, extra):
                    kind, n = tile[0], tile[1]
                    bank = ps_m[:, plan.bank[tile], :] if tile in plan.at else None
                    h = n % HG
                    if tile in plan.hi_at:
                        dve.wait_ge(hi_done, his + plan.hi_at[tile] + 1)
                    if kind == "X":
                        lo(xT[:, n % 2, LO, tile[2], :], xT[:, n % 2, HI, tile[2], :], bank, None)
                        if plan is FIRST and n == 0 and tile[2] == KT - 1:
                            add_ada(2)
                            add_ada(3)
                    elif kind == "K":
                        lo(QK[:, 1, LO, :], QK[:, 1, HI, :], bank, group_cols[:, HG + h:HG + h + 1])
                        if plan is FIRST and n == 0:
                            add_ada(4)
                            add_ada(5)
                    elif kind == "Q":
                        lo(QK[:, 0, LO, :], QK[:, 0, HI, :], bank, group_cols[:, h:h + 1])
                    elif kind == "V":
                        lo(V[:, LO, tile[2], :], V[:, HI, tile[2], :], bank, None)
                        if plan is FIRST and n == 0 and tile[2] == 1:
                            ada_columns(1)
                    elif kind == "O":
                        lo(O[:, LO, h, :], O[:, HI, h, :], bank, group_cols[:, 2 * HG + h:2 * HG + h + 1])
                    elif kind == "Y":
                        at = TT * n + tile[2]
                        dve.wait_ge(m_done, base + plan.at[tile] + 1)
                        if plan is FIRST and tile[2] == 0:
                            dve.wait_ge(acc_init[n], 16 * TT)
                        v.tensor_tensor(acc[:, at, :], acc[:, at, :], bank, ALU.add).then_inc(m_free, 1)
                    elif kind == "S":
                        s = TT * n + tile[2]
                        dve.wait_ge(s_done, NS * g + s + 1)
                        v.tensor_reduce(neg_max[:, s % TT:s % TT + 1], ps_s[:, s % 2, :], axis=AX_X, op=ALU.max,
                                        negate=True).then_inc(max_done, 1)
                        if tile[2] >= 1:
                            inverse(g, s - 1)
                        if tile[2] == TT - 1:
                            inverse(g, s)
                    elif kind == "C":
                        j = tile[2]
                        dve.wait_ge(c_hi, NS * g + TT * n + j + 1)
                        v.tensor_tensor(probT[:, LO, j, :], ps_c[:, (TT * n + j) % 2, :], f(probT[:, HI, j, :]),
                                        ALU.subtract).then_inc(c_lo, 1)
                    else:
                        norm_step(0 if plan is FIRST else 1, tile)

            group(0)
            with dve.Fori(1, G - 1) as g:
                group(g)
            group(G - 1)
            for tile in after(MLP_PLAN.done, MLP_EXTRA):
                kind, u = tile[0], tile[1]
                bank = ps_m[:, MLP_PLAN.bank[tile], :] if tile in MLP_PLAN.at else None
                if kind == "X":
                    dve.wait_ge(hi_done, HI_MLP + MLP_PLAN.hi_at[tile] + 1)
                    lo(xT[:, u % 2, LO, tile[2], :], xT[:, u % 2, HI, tile[2], :], bank, None)
                elif kind == "H":
                    j = tile[2]
                    n = 4 * u + j
                    dve.wait_ge(gelu_done, n + 1)
                    v.tensor_copy(hid[u % 2][:, HI, j, :], prob[:, j, :]).then_inc(h_hi, 1)
                    dve.wait_ge(h_hi, n + 1)
                    v.tensor_tensor(hid[u % 2][:, LO, j, :], prob[:, j, :], f(hid[u % 2][:, HI, j, :]),
                                    ALU.subtract).then_inc(h_lo, 1)
                elif kind == "Z":
                    b, i = u % B, tile[2]
                    a = acc[:, TT * b + i, :]
                    dve.wait_ge(m_done, M_MLP + MLP_PLAN.at[tile] + 1)
                    if u < B and i == 0:
                        dve.wait_ge(acc_init[b], 2 * 16 * TT)
                    v.tensor_tensor(a, a, bank, ALU.add).then_inc(m_free, 1)
                    if u >= B * JG - B:
                        dve.wait_ge(m_free, M_MLP + MLP_PLAN.at[tile] + 1)
                        if i == 0:
                            dve.wait_ge(wide_loaded[b % 2], 16 * (2 + b // 2 + 1))
                            dve.wait_ge(xx_loaded[b % 2], 16 * (b // 2 + 1))
                        link(v.tensor_tensor(a, a, wide[:, b % 2, :], ALU.mult))
                        v.tensor_tensor(a, a, xx_in[:, b % 2, i, :], ALU.add).then_inc(fin_done, 1)
                else:
                    norm_step(1, tile)

        @block.tensor
        def _(pe):
            mm, tr = nc.tensor.matmul, nc.tensor.transpose
            pe.wait_ge(consts, 1)
            pe.wait_ge(small_loaded, 48)
            tr(ps_m[:, 0, 0:64], bias_rows[:, :], ident[0:64, 0:64])
            for k in range(KT):
                last = tr(ps_m[:, 1, B * k:B * k + B], cond_sb[:, P * k:P * k + P], ident[0:B, 0:B])
            last.then_inc(pro_cols, 1)
            for b in range(B):
                pe.wait_ge(token_sums, b + 1)
                at = NBLK * (B - 1 - b)
                last = mm(ps_m[0:32, 2, :], block_ind[:, at:at + 32], raw2[:, b, :], start=(b == 0), stop=(b == B - 1))
            last.then_inc(pro_blocks, 1)

            def transpose_weights(m):
                pe.wait_ge((wk_loaded, wo_loaded)[m], 16)
                for k in range(KT):
                    if m:
                        pe.wait_ge(wT_sb, k + 1)
                    for r in range(KT):
                        last = tr(four[k][:, P * r:P * r + P], (Wk_sb, Wo_sb)[m][:, r, P * k:P * k + P], ident[:, :])
                    last.then_inc(wT_psum, 1)

            transpose_weights(0)
            pe.wait_ge(pro_blocks_sb, 1)
            for k in range(KT):
                last = tr(ps_m[:, 3, 32 * k:32 * k + 32], blocks[:, P * k:P * k + P], ident[0:32, 0:32])
            last.then_inc(pro_blocksT, 1)
            pe.wait_ge(pro_blocksT_sb, 1)
            pe.wait_ge(pro_condT, 1)
            pe.wait_ge(wT_sb, KT)
            for k in range(KT):
                last = mm(ps_m[0:32, 0, :], blocksT[:, k, :], WkT[:, k, :], start=(k == 0), stop=(k == KT - 1))
            last.then_inc(pro_keys, 1)
            transpose_weights(1)
            pe.wait_ge(score_col, 1)
            tr(ps_m[0:1, 1, 64:96], small[:, 4:5], ident[0:32, 0:32]).then_inc(score_row, 1)
            pe.wait_ge(attn_row, 1)
            mm(ps_m[0:32, 1, 100:101], small_row[:, 64:96], ones[:, 0:1], start=True, stop=True).then_inc(attn_col, 1)
            pe.wait_ge(attn_mask, 1)
            for k in range(KT):
                last = mm(ps_m[:, 1, 128 + B * k:128 + B * k + B], blocks[:, P * k:P * k + P], small[:, 8:12],
                          start=True, stop=True)
            last.then_inc(att_psum, 1)
            pe.wait_ge(att_copied, 1)
            pe.wait_ge(wT_sb, 2 * KT)
            for k in range(KT):
                last = mm(ps_m[0:B, 2, :], att_sb[:, B * k:B * k + B], WoT[:, k, :], start=(k == 0), stop=(k == KT - 1))
            last.then_inc(proj_psum, 1)
            pe.wait_ge(proj_sb, 1)
            mm(ps_m[:, 0, :], ones[:, :], proj_rows[0:1, :], start=True, stop=True).then_inc(proj_bc, 1)

            def ada_chunk(c):
                pe.wait_ge(adaw_loaded[c], 16)
                if c >= 4:
                    pe.wait_ge(ada_sb, c - 3)
                for k in range(KT):
                    last = mm(four[c % 4][0:B, :], condT[:, k, :], ada_buf[c][:, k, :],
                              start=(k == 0), stop=(k == KT - 1))
                last.then_inc(ada_psum, 1)

            def ada_transpose(half):
                pe.wait_ge(ada_sb, 2 if half == 0 else 6)
                for y in range(2):
                    for k in range(KT):
                        at, part = 16 * y + B * k, 3 * half + y
                        last = tr(adaT_bank[half][:, at:at + B], ada[:, 512 * part + P * k:512 * part + P * k + P],
                                  ident[0:B, 0:B])
                last.then_inc(adaT_psum, 1)

            for c in range(3):
                ada_chunk(c)
            ada_transpose(0)
            ada_chunk(3)
            ada_chunk(4)
            ada_chunk(5)

            def product(out_ap, stationary, moving, k0, k1, last_k, before_lo=None):
                for k in range(k0, k1):
                    for n, (a, c) in enumerate(PAIRS):
                        if a == LO and before_lo is not None:
                            before_lo()
                        last = mm(out_ap, stationary(a, k), moving(c, k), start=(k == 0 and n == 0),
                                  stop=(k == last_k - 1 and n == len(PAIRS) - 1))
                return last

            def transpose_x(stage, b, k, bank):
                if k == 0:
                    pe.wait_ge(hat_done, TT * (B * stage + b + 1))
                for i in range(TT):
                    last = tr(bank[:, P * i:P * i + P], hat_tile(stage, b, i)[:, P * k:P * k + P], ident[:, :])
                last.then_inc(m_done, 1)

            def group(g):
                plan, base = plan_of(g), m_base(g)
                for s in plan.order:
                    kind, n = s[0], s[1]
                    b, h = n // HG, n % HG
                    xb = xT[:, (b if kind in "KQ" else n) % 2]
                    tile = ("O", n) if kind == "D" else s[:2] if kind in "KQ" else s[:3]
                    if tile in plan.at:
                        bank = ps_m[:, plan.bank[tile], :]
                        first = s[2] == 0 if kind in "KQD" else s[3] == 0 if kind == "Y" else True
                        if first and tile in plan.need:
                            pe.wait_ge(m_free, base + plan.need[tile])
                    if kind == "X":
                        if plan is FIRST and n == 0 and s[2] == 0:
                            pe.wait_ge(ada_cols_sb, 2)
                        transpose_x(0 if plan is FIRST else 1, n, s[2], bank)
                    elif kind in "KQ":
                        if s[2] == 0 and h == 0 and kind == "K":
                            if plan is FIRST and b:
                                pe.wait_ge(m_free, plan.at[("X", b, KT - 1)] + 1)
                            elif plan is not FIRST:
                                pe.wait_ge(xT_loaded[b % 2], 16 * (2 * (g - 1) + b // 2 + 1))
                        mat = MK if kind == "K" else MQ
                        if s[2] == 0 and b == 0:
                            pe.wait_ge(w_split, 16 * g + (4 if kind == "K" else 8) + h + 1)
                        by_tile = plan is FIRST and tile == ("K", 0)
                        for k in range(s[2], s[3]) if by_tile else [None]:
                            if by_tile:
                                pe.wait_ge(m_free, plan.at[("X", b, k)] + 1)
                            last = product(bank, lambda a, k: W[:, mat, a, k, P * h:P * h + P],
                                           lambda c, k: xb[:, c, k, :],
                                           *((k, k + 1) if by_tile else s[2:4]), KT)
                        if s[3] == KT:
                            last.then_inc(m_done, 1)
                    elif kind == "V":
                        j = s[2]
                        product(bank, lambda a, k: xb[:, a, k, P * j:P * j + P],
                                lambda c, k: W[:, MV, c, k, :], 0, KT, KT).then_inc(m_done, 1)
                        if plan is FIRST and n == 0 and j == 1:
                            ada_transpose(1)
                    elif kind == "Y":
                        i = s[2]
                        if i == 0:
                            if s[3] == 0:
                                pe.wait_ge(w_split, 16 * g + 16)
                            pe.wait_ge(m_free, base + plan.at[("O", HG * n + s[4] - 1)] + 1)
                        last = product(bank, lambda a, k: O[:, a, k, P * i:P * i + P],
                                       lambda c, k: W[:, MO, c, k, :], s[3], s[4], HG)
                        if s[4] == HG:
                            last.then_inc(m_done, 1)
                    elif kind == "S":
                        t = s[2]
                        q_lo = None
                        if t == 0:
                            pe.wait_ge(m_free, base + plan.at[("K", n)] + 1)
                            pe.wait_ge(hi_done, hi_base(g) + plan.hi_at[("Q", n)] + 1)

                            def q_lo():
                                pe.wait_ge(m_free, base + plan.at[("Q", n)] + 1)

                        if plan is FIRST and n == 0 and t == 0:
                            pe.wait_ge(ada_sb, 6)
                        if TT * n + t >= 2:
                            pe.wait_ge(exp_done, NS * g + TT * n + t - 1)
                        product(ps_s[:, (TT * n + t) % 2, :], lambda a, k: QK[:, 0, a, P * t:P * t + P],
                                lambda c, k: QK[:, 1, c, :], 0, 1, 1, q_lo).then_inc(s_done, 1)
                    elif kind == "C":
                        j = s[2]
                        if j == 0:
                            if plan is FIRST and n == 0:
                                pe.wait_ge(ada_cols_sb, 3)
                            pe.wait_ge(norm_done, NS * g + TT * n + TT)
                        if TT * n + j >= 2:
                            pe.wait_ge(c_lo, NS * g + TT * n + j - 1)
                        for t in range(TT):
                            last = tr(ps_c[:, (TT * n + j) % 2, P * t:P * t + P], prob[:, t, P * j:P * j + P],
                                      ident[:, :])
                        last.then_inc(c_done, 1)
                    elif kind == "D":
                        j = s[2]
                        if j == 0 and h == 0:
                            pe.wait_ge(m_free, base + plan.at[("V", b, TT - 1)] + 1)
                        pe.wait_ge(c_lo, NS * g + TT * n + j + 1)
                        last = product(bank, lambda a, k: V[:, a, k, P * h:P * h + P],
                                       lambda c, k: probT[:, c, k, :], j, j + 1, TT)
                        if j == TT - 1:
                            last.then_inc(m_done, 1)

            group(0)
            with pe.Fori(1, G - 1) as g:
                group(g)
            group(G - 1)
            for s in MLP_PLAN.order:
                kind, u = s[0], s[1]
                b, jg = u % B, u // B
                if s in MLP_PLAN.at:
                    bank = ps_m[:, MLP_PLAN.bank[s], :]
                    pe.wait_ge(m_free, M_MLP + MLP_PLAN.need[s])
                if kind == "X":
                    transpose_x(1, u, s[2], bank)
                elif kind == "H":
                    j = s[2]
                    n = 4 * u + j
                    w1 = FFN_AT[jg][0]
                    if j == 0 and u < 2:
                        pe.wait_ge(m_free, m_base(G - 1) + LAST.at[("X", u, KT - 1)] + 1)
                    elif j == 0 and u < B:
                        pe.wait_ge(m_free, M_MLP + MLP_PLAN.at[("X", u, KT - 1)] + 1)
                    elif j == 0:
                        pe.wait_ge(xT_loaded[b % 2], 16 * (2 * (G - 1) + 2 * (jg - 1) + b // 2 + 1))
                    if b == 0:
                        pe.wait_ge(w_split, 4 * (R_MLP + 2 * jg) + j + 1)
                    if n >= 4:
                        pe.wait_ge(gelu_done, n - 3)
                    product(four[j], lambda a, k: W[:, w1, a, k, P * j:P * j + P],
                            lambda c, k: xT[:, b % 2, c, k, :], 0, KT, KT).then_inc(h_done, 1)
                else:
                    i = s[2]
                    w2 = FFN_AT[jg][1]
                    if i == 0:
                        pe.wait_ge(h_lo, 4 * u + 4)
                        if b == 0:
                            pe.wait_ge(w_split, 4 * (R_MLP + 2 * jg + 2))
                    product(bank, lambda a, k: hid[u % 2][:, a, k, P * i:P * i + P],
                            lambda c, k: W[:, w2, c, k, :], 0, 4, 4).then_inc(m_done, 1)


_INS = ["x", "cond_2048", "L0_cond_rms_weight", "L0_cond_Wk", "L0_cond_Wo", "L0_cond_ln_gamma", "L0_cond_ln_beta",
        "L1_cond_ada_w", "L1_cond_ada_b", "L1_cond_qkv_w", "L1_cond_qkv_b", "L1_cond_out_w", "L1_cond_out_b",
        "L1_cond_ffn_w1", "L1_cond_ffn_b1", "L1_cond_ffn_w2", "L1_cond_ffn_b2"]


def kernel(**inputs):
    import numpy as _np
    import concourse.bacc as _bacc
    from concourse import mybir as _mybir
    from concourse.bass_utils import run_bass_kernel_spmd as _run

    nc = _bacc.Bacc("TRN2", target_bir_lowering=False, num_devices=1)
    arrays, args = {}, []
    for name in _INS:
        a = _np.ascontiguousarray(inputs[name])
        arrays[f"in_{name}"] = a
        args.append(nc.dram_tensor(f"in_{name}", a.shape, _mybir.dt.from_np(a.dtype), kind="ExternalInput").ap())
    out = nc.dram_tensor("out_0", (B, S, D), F32, kind="ExternalOutput").ap()
    build(nc, *args, out)
    r = _run(nc, [arrays], core_ids=[0])
    return r.results[0]["out_0"]
```
